# Optimizing a Trainium2 kernel written in Bass

```python
import numpy as np
import jax
import jax.numpy as jnp

def _softmax(x, axis=-1):
    return jax.nn.softmax(x, axis=axis)

def _gelu(x):
    return jax.nn.gelu(x, approximate=True)

def _silu(x):
    return jax.nn.silu(x)

def _sigmoid(x):
    return jax.nn.sigmoid(x)

def _layernorm(x, axis=-1, eps=1e-05):
    m = jnp.mean(x, axis=axis, keepdims=True)
    v = jnp.var(x, axis=axis, keepdims=True)
    return (x - m) / jnp.sqrt(v + eps)

def _scatter_add(tgt, idx, src, axis=0):
    return tgt.at[idx].add(src)

def _segment_sum(src, seg, n):
    return jax.ops.segment_sum(src, seg, n)
kernel_name = 'mk_adj_ffn_d1_adj_r2_c2c053'

def setup_inputs(seed: int=0):
    np.random.seed(seed)
    _w = jnp.asarray

    def _rec_inputs():
        import jax
        import jax.numpy as jnp
        _gk = jax.random.key(seed)
        x = -0.000929 + 1 * jax.random.normal(jax.random.fold_in(_gk, 1), (2048, 128), jnp.float32)
        _a = jax.random.bernoulli(jax.random.fold_in(_gk, 2), 0.00195312, (2048, 2048))
        _a = jnp.logical_or(_a, jnp.swapaxes(_a, -1, -2))
        _a = jnp.logical_or(_a, jnp.eye(2048, dtype=bool))
        _af = _a.astype(jnp.float32)
        adj = _af
        return (x, adj)
    x, adj = _rec_inputs()

    def _L0_gnn_setup():
        import jax, jax.numpy as jnp
        import numpy as np
        ALPHA = 0.2
        NEG_INF = -9000000000000000.0
        LN_EPS = 1e-05
        N = 2048
        IN_F = 128
        OUT_F = 128
        HEADS = 4
        HEAD_DIM = OUT_F // HEADS
        EDGE_PROB = 0.02
        key = jax.random.key(seed)
        kx, ka, kw, kav = jax.random.split(key, 4)
        x = jax.random.normal(kx, (N, IN_F), dtype=jnp.float32)
        adj = jax.random.bernoulli(ka, EDGE_PROB, (N, N)).astype(jnp.float32)
        adj = jnp.maximum(adj, jnp.eye(N, dtype=jnp.float32))

        def xavier(k, shape, gain=1.414):
            fan_in, fan_out = (shape[0], shape[1])
            bound = gain * np.sqrt(6.0 / (fan_in + fan_out))
            return jax.random.uniform(k, shape, jnp.float32, -bound, bound)
        W = xavier(kw, (IN_F, OUT_F))
        a = xavier(kav, (2 * HEAD_DIM, 1))
        gamma = jnp.ones((OUT_F,), dtype=jnp.float32)
        beta = jnp.zeros((OUT_F,), dtype=jnp.float32)
        return {'x': x, 'adj': adj, 'W': W, 'a': a, 'gamma': gamma, 'beta': beta}
    _L0_gnn_all = _L0_gnn_setup()
    _L0_gnn_in = {k: v for k, v in _L0_gnn_all.items() if k in ('W', 'a', 'gamma', 'beta')}
    del _L0_gnn_all

    def _L0_ffn_setup():
        import jax, jax.numpy as jnp
        import numpy as np
        DIM = 128
        HEADS = 8
        NUM_KEYS = 128
        NUM_KV = NUM_KEYS ** 2
        PK_TOPK = 16
        FINAL_TOPK = 16
        DIM_KEY = DIM // 2
        P = 2

        def _pk(x, Wq_pk, pk_keys):
            b, n, _ = x.shape
            q = (x @ Wq_pk).reshape(b, n, P, HEADS, DIM_KEY).transpose(2, 0, 1, 3, 4)
            sim = jnp.einsum('pbnhd,pkhd->pbnhk', q, pk_keys)
            scores, idx = jax.lax.top_k(sim, PK_TOPK)
            idx0 = idx[0]
            idx1 = idx[1] * NUM_KEYS
            index = (idx0[..., :, None] + idx1[..., None, :]).reshape(b, n, HEADS, PK_TOPK * PK_TOPK)
            score = (scores[0][..., :, None] + scores[1][..., None, :]).reshape(b, n, HEADS, PK_TOPK * PK_TOPK)
            final_scores, pk_idx = jax.lax.top_k(score, FINAL_TOPK)
            final_indices = jnp.take_along_axis(index, pk_idx, axis=-1)
            final_scores = jax.nn.softmax(final_scores, axis=-1)
            return (final_scores, final_indices)
        key = jax.random.key(seed)
        ks = jax.random.split(key, 7)
        b, n = (2, 512)
        std = 0.02
        x = jax.random.normal(ks[0], (b, n, DIM), dtype=jnp.float32)
        Wq_pk = jax.random.normal(ks[1], (DIM, P * HEADS * DIM_KEY), dtype=jnp.float32) * std
        pk_keys = jax.random.normal(ks[2], (P, NUM_KEYS, HEADS, DIM_KEY), dtype=jnp.float32) * std
        Wq = jax.random.normal(ks[3], (DIM, HEADS * DIM), dtype=jnp.float32) * std
        keys_table = jax.random.normal(ks[4], (NUM_KV * HEADS, DIM), dtype=jnp.float32) * std
        values_table = jax.random.normal(ks[5], (NUM_KV * HEADS, DIM), dtype=jnp.float32) * std
        Wo = jax.random.normal(ks[6], (DIM * HEADS, DIM), dtype=jnp.float32) * std
        return {'x': x, 'Wq_pk': Wq_pk, 'pk_keys': pk_keys, 'Wq': Wq, 'keys_table': keys_table, 'values_table': values_table, 'Wo': Wo}
    _L0_ffn_all = _L0_ffn_setup()
    _L0_ffn_in = {k: v for k, v in _L0_ffn_all.items() if k in ('Wq_pk', 'pk_keys', 'Wq', 'keys_table', 'values_table', 'Wo')}
    del _L0_ffn_all
    return {'x': x, 'adj': adj, 'L0_gnn_W': _L0_gnn_in['W'], 'L0_gnn_a': _L0_gnn_in['a'], 'L0_gnn_gamma': _L0_gnn_in['gamma'], 'L0_gnn_beta': _L0_gnn_in['beta'], 'L0_ffn_Wq_pk': _L0_ffn_in['Wq_pk'], 'L0_ffn_pk_keys': _L0_ffn_in['pk_keys'], 'L0_ffn_Wq': _L0_ffn_in['Wq'], 'L0_ffn_keys_table': _L0_ffn_in['keys_table'], 'L0_ffn_values_table': _L0_ffn_in['values_table'], 'L0_ffn_Wo': _L0_ffn_in['Wo']}

def reference(x, adj, L0_gnn_W, L0_gnn_a, L0_gnn_gamma, L0_gnn_beta, L0_ffn_Wq_pk, L0_ffn_pk_keys, L0_ffn_Wq, L0_ffn_keys_table, L0_ffn_values_table, L0_ffn_Wo):
    import jax
    import jax.numpy as jnp

    def _L0_gnn_ref(x, adj, W, a, gamma, beta):
        import jax, jax.numpy as jnp
        import numpy as np
        ALPHA = 0.2
        NEG_INF = -9000000000000000.0
        LN_EPS = 1e-05
        N = 2048
        IN_F = 128
        OUT_F = 128
        HEADS = 4
        HEAD_DIM = OUT_F // HEADS
        EDGE_PROB = 0.02
        n = x.shape[0]
        head_dim = a.shape[0] // 2
        heads = W.shape[1] // head_dim
        h = (x @ W).reshape(n, heads, head_dim)
        src = jnp.einsum('nhd,d->nh', h, a[:head_dim, 0])
        dst = jnp.einsum('nhd,d->nh', h, a[head_dim:, 0])
        e = src[:, :, None] + dst.T[None, :, :]
        e = jnp.where(e > 0, e, ALPHA * e)
        mask = adj[:, None, :] > 0
        e = jnp.where(mask, e, NEG_INF)
        attn = jax.nn.softmax(e, axis=-1)
        out = jnp.einsum('nhm,mhd->nhd', attn, h)
        out = out.reshape(n, heads * head_dim)
        mu = jnp.mean(out, axis=-1, keepdims=True)
        var = jnp.var(out, axis=-1, keepdims=True)
        out = (out - mu) / jnp.sqrt(var + LN_EPS) * gamma + beta
        return out

    def _L0_ffn_ref(x, Wq_pk, pk_keys, Wq, keys_table, values_table, Wo):
        import jax, jax.numpy as jnp
        import numpy as np
        DIM = 128
        HEADS = 8
        NUM_KEYS = 128
        NUM_KV = NUM_KEYS ** 2
        PK_TOPK = 16
        FINAL_TOPK = 16
        DIM_KEY = DIM // 2
        P = 2

        def _pk(x, Wq_pk, pk_keys):
            b, n, _ = x.shape
            q = (x @ Wq_pk).reshape(b, n, P, HEADS, DIM_KEY).transpose(2, 0, 1, 3, 4)
            sim = jnp.einsum('pbnhd,pkhd->pbnhk', q, pk_keys)
            scores, idx = jax.lax.top_k(sim, PK_TOPK)
            idx0 = idx[0]
            idx1 = idx[1] * NUM_KEYS
            index = (idx0[..., :, None] + idx1[..., None, :]).reshape(b, n, HEADS, PK_TOPK * PK_TOPK)
            score = (scores[0][..., :, None] + scores[1][..., None, :]).reshape(b, n, HEADS, PK_TOPK * PK_TOPK)
            final_scores, pk_idx = jax.lax.top_k(score, FINAL_TOPK)
            final_indices = jnp.take_along_axis(index, pk_idx, axis=-1)
            final_scores = jax.nn.softmax(final_scores, axis=-1)
            return (final_scores, final_indices)
        b, n, d = x.shape
        q = (x @ Wq).reshape(b, n, HEADS, DIM) * DIM ** (-0.5)
        kv_scores, indices = _pk(x, Wq_pk, pk_keys)
        offsets = jnp.arange(HEADS, dtype=indices.dtype) * NUM_KV
        ind = indices + offsets[None, None, :, None]
        k = jnp.einsum('bnhk,bnhkd->bnhd', kv_scores, keys_table[ind])
        v = jnp.einsum('bnhk,bnhkd->bnhd', kv_scores, values_table[ind])
        sim = jnp.einsum('bihd,bjhd->bhij', q, k)
        neg = -jnp.finfo(sim.dtype).max
        causal = jnp.tril(jnp.ones((n, n), dtype=bool))
        sim = jnp.where(causal, sim, neg)
        attn = jax.nn.softmax(sim, axis=-1)
        out = jnp.einsum('bhij,bjhd->bhid', attn, v)
        out = out.transpose(0, 2, 1, 3).reshape(b, n, HEADS * DIM)
        return out @ Wo
    x = x + _L0_gnn_ref(_layernorm(x, axis=-1), adj, L0_gnn_W, L0_gnn_a, L0_gnn_gamma, L0_gnn_beta)
    x = x + _L0_ffn_ref(_layernorm(x, axis=-1)[None], L0_ffn_Wq_pk, L0_ffn_pk_keys, L0_ffn_Wq, L0_ffn_keys_table, L0_ffn_values_table, L0_ffn_Wo)[0]
    return x

_drawn_inputs = setup_inputs


def setup_inputs(seed=0):
    import zlib

    import numpy as np

    out = dict(_drawn_inputs(seed))
    spreads = {'L0_gnn_gamma': (1.0, 0.2), 'L0_gnn_beta': (0.0, 0.1)}
    factors = {'L0_ffn_Wq_pk': 34.08,
     'L0_ffn_pk_keys': 34.317,
     'L0_ffn_Wq': 64.0,
     'L0_ffn_keys_table': 64.0,
     'L0_ffn_values_table': 30.764,
     'L0_ffn_Wo': 30.496}
    for name, (base, spread) in spreads.items():
        noise = np.random.default_rng([zlib.crc32(name.encode()), seed]).standard_normal(out[name].shape)
        drawn = base * np.exp(spread * noise) if base else spread * noise
        out[name] = jnp.asarray(drawn.astype(out[name].dtype))
    for name, factor in factors.items():
        out[name] = (out[name] * factor).astype(out[name].dtype)
    return out
```

```python
from contextlib import ExitStack

import concourse.bass as bass
from concourse import mybir

F32 = mybir.dt.float32
BF16 = mybir.dt.bfloat16
U32 = mybir.dt.uint32
ALU = mybir.AluOpType
ACT = mybir.ActivationFunctionType
AX_X = mybir.AxisListType.X

P = 128
N = 2048
NT = N // P
D = 128
GH, GD = 4, 32
MH = 8
NKEYS = 128
DKEY = 64
TOPK = 16
BANK = 512
ALPHA = 0.2
LN_EPS = 1e-5
MASKED = -9.0e15 / ALPHA
LOWEST = -3.0e38
RECTS = [(0, 1, 16), (1, 1, 8), (2, 2, 5), (4, 4, 3), (8, 8, 1)]
NC = sum(a * b for _, a, b in RECTS)
SPANS = [(0, 4, 1, 1), (4, 7, 1, 1), (7, 8, 0, 1), (8, 12, 0, 1), (12, 15, 0, 1), (15, 16, 0, 0)]
C_IDENT, C_CAUSAL, C_IOTA = 0, P, P + BANK + 3 * P
C_THIRDS = C_IOTA + NC
C_END = C_THIRDS + 6


class Tally:

    def __init__(self, start=0):
        self.base, self.n, self.t, self.first, self.per = start, 0, None, 0, 0

    def enter(self, t, first, per):
        self.t, self.first, self.per = t, first, per

    def leave(self, bodies):
        assert self.n in (0, self.per), (self.n, self.per)
        self.base += self.per * bodies
        self.n, self.t = 0, None

    def up(self, k=1):
        self.n += k
        return self.now()

    def now(self):
        if self.t is None:
            return self.base + self.n
        if isinstance(self.t, int):
            return self.base + self.n + (self.t - self.first) * self.per
        return self.t * self.per + (self.base + self.n - self.first * self.per)


def per_body(graph, nxt, chunks):
    pieces = 2 * GH * graph
    return dict(
        x_ready=8 * pieces + MH * chunks, x_free_dve=4 * pieces, x_free_act=4 * pieces + MH * chunks,
        c_ready=2 + 5 * nxt + pieces + MH, c_free_act=2 + 5 * nxt + MH, c_free_dve=pieces,
        pt_used=4 * pieces + MH * chunks, u_free=pieces, u_ready=pieces, gexp_ready=pieces,
        lt_ready=2 * graph, adj_free=2 * graph, s_ready=MH, max_ready=MH, aexp_ready=MH,
        acc_ready=MH, kv_ready=2 * MH, ot_ready=MH, otc_ready=MH, y_ready=MH, y_free=MH,
        top_ready=MH * nxt, w_ready=MH * nxt, idx_ready=MH * nxt, sim_ready=4 * nxt,
        sim_free=4 * nxt, var_ready=nxt + 2 * graph, std_ready=nxt + 2 * graph, xn2_ready=nxt,
        xn2t_ready=nxt, qt_ready=2, res_ready=1, row_free=4 * MH,
    )


def build(nc, x, adj, w, w_t, a_blk, gamma, beta, wqpk, keys, wq, kv, wo, const, out):
    with ExitStack() as ctx:
        def sb(name, shape, dt=F32):
            return ctx.enter_context(nc.sbuf_tensor(name, shape, dt))

        def ps(name, shape):
            return ctx.enter_context(nc.psum_tensor(name, shape, F32))

        def sem(name):
            return ctx.enter_context(nc.semaphore(name))

        k_t = sb("k_t", [P, 4, MH, BANK])
        v = sb("v", [P, NT, MH, D])
        rows = sb("rows", [P, TOPK, 2 * D])
        wcomb = sb("wcomb", [P, MH * 2 * NKEYS])
        wq_s = sb("wq_s", [P, MH * D])
        wo_s = sb("wo_s", [P, MH, D])
        x1 = sb("x1", [P, NT, D])
        prob = sb("prob", [P, N])
        pt = sb("pt", [P, 2, BANK])
        sim = sb("sim", [P, 2, 2, 2, NKEYS])
        q_t = sb("q_t", [P, MH, P])
        cst = sb("cst", [P, C_END])
        gam = sb("gam", [P, D])
        bet = sb("bet", [P, D])
        cmask = sb("cmask", [P, BANK])
        acc = sb("acc", [P, 2, 2 * D])
        o_t = sb("o_t", [P, P])
        xn2 = sb("xn2", [P, D])
        xn2_t = sb("xn2_t", [P, P])
        gout = sb("gout", [P, D])
        best = sb("best", [P, 2, TOPK])
        besti = sb("besti", [P, 2, TOPK], U32)
        bestf = sb("bestf", [P, 2, TOPK])
        rest = sb("rest", [P, NKEYS])
        csum = sb("csum", [P, NC])
        cidx = sb("cidx", [P, NC])
        crest = sb("crest", [P, NC])
        top = sb("top", [P, 2, TOPK])
        pos = sb("pos", [P, TOPK], U32)
        posf = sb("posf", [P, TOPK])
        hot = sb("hot", [P, TOPK, NC])
        idxf = sb("idxf", [P, TOPK])
        idx = sb("idx", [P, MH, TOPK], U32)
        wgt = sb("wgt", [P, MH, TOPK])
        stat = sb("stat", [P, 8])
        mv = sb("mv", [P, 2])
        std = sb("std", [P, 2])
        small = sb("small", [P, 32])
        mvx = sb("mvx", [P, NT, 2])
        stdx = sb("stdx", [P, NT])
        k_hi = k_t[:, 2:4].rearrange("p q h c -> p (q h c)")
        v_hi = v[:, NT // 2:NT].rearrange("p t h d -> p (t h d)")
        xn_t = k_hi[:, 0:N]
        h_all = k_hi[:, N:2 * N].rearrange("p (t d) -> p t d", t=NT)
        r_src = k_hi[:, 2 * N:2 * N + N // 2].bitcast(BF16)
        r_dst = k_hi[:, 2 * N + N // 2:3 * N].bitcast(BF16)
        wrow = k_hi[:, 3 * N:3 * N + 2 * P].rearrange("p (a b) -> p a b", a=2)
        src_t = k_hi[:, 3 * N + 2 * P:3 * N + 2 * P + P // 2].bitcast(BF16)
        w_s = k_hi[:, 3 * N + 3 * P:3 * N + 4 * P]
        wt_s = k_hi[:, 3 * N + 4 * P:3 * N + 5 * P]
        ab_s = k_hi[:, 3 * N + 5 * P:3 * N + 5 * P + 8]
        wa_s = k_hi[:, 3 * N + 5 * P + 8:3 * N + 5 * P + 16]
        part = k_hi[:, 3 * N + 6 * P:3 * N + 8 * P].bitcast(BF16)
        u = [v_hi[:, 0:N], v_hi[:, N:2 * N]]
        adj_s = [v_hi[:, 2 * N:3 * N], v_hi[:, 3 * N:4 * N]]
        wqpk_s = v_hi[0:DKEY, 0:N]
        keys_s = v_hi[0:DKEY, N:2 * N]
        xn = prob
        resid = pt[:, 0, :]

        ident = cst[:, C_IDENT:C_IDENT + P]
        iota = cst[:, C_IOTA:C_IOTA + NC]
        src_cols = [cst[:, C_THIRDS + i:C_THIRDS + i + 1] for i in range(3)]
        dst_cols = [cst[:, C_THIRDS + i:C_THIRDS + i + 1] for i in range(3, 6)]

        p_s = ps("p_s", [P, 4 * BANK])
        p_x = ps("p_x", [P, 2, BANK])
        p_c = ps("p_c", [P, BANK])
        p_o = ps("p_o", [P, BANK])

        names = list(per_body(1, 1, 1))
        S = {n: sem(n) for n in names}
        row_in = [sem(f"row_in{k}") for k in range(TOPK)]
        adj_in = [sem(f"adj_in{k}") for k in range(2)]
        ld_x, ld_w, ld_pk, ld_c, ld_late = sem("ld_x"), sem("ld_w"), sem("ld_pk"), sem("ld_c"), sem("ld_late")
        out_done = sem("out_done")
        pool_zero = sem("pool_zero")
        dve_step, act_step = sem("dve_step"), sem("act_step")
        pro_pe, pro_act, pro_dve = sem("pro_pe"), sem("pro_act"), sem("pro_dve")

        x_v = x.rearrange("(t p) d -> p t d", p=P)
        out_v = out.rearrange("(t p) d -> p t d", p=P)
        adj_v = adj.rearrange("(t p) m -> p t m", p=P)

        START = dict(u_free=2, kv_ready=4, sim_free=2, row_free=4, y_free=1, pt_used=2)

        def tallies():
            return {n: Tally(START.get(n, 0)) for n in names}

        def over_tiles(eng, T, body):
            for first, end, graph, nxt in SPANS:
                chunks = first // 4 + 1
                per = per_body(graph, nxt, chunks)
                if end - first == 1:
                    for n in names:
                        T[n].enter(first, first, per[n])
                    body(first, graph, nxt, chunks)
                else:
                    with eng.Fori(first, end) as t:
                        for n in names:
                            T[n].enter(t, first, per[n])
                        body(t, graph, nxt, chunks)
                for n in names:
                    T[n].leave(end - first)

        block = ctx.enter_context(nc.Block())

        @block.sync
        def _(sp):
            T = tallies()
            sp.dma_start(x1[:], x_v).then_inc(ld_x, 16)
            sp.dma_start(wt_s, w_t).then_inc(ld_w, 16)
            sp.dma_start(ab_s, a_blk).then_inc(ld_w, 16)
            sp.dma_start(w_s, w).then_inc(ld_w, 16)
            for i in range(2):
                sp.dma_start(adj_s[i], adj_v[:, i, :]).then_inc(adj_in[i], 16)
            sp.dma_start(gam[:], gamma.partition_broadcast(P)).then_inc(ld_late, 16)
            sp.dma_start(bet[:], beta.partition_broadcast(P)).then_inc(ld_late, 16)
            sp.dma_start(wq_s[:], wq).then_inc(ld_late, 16)
            sp.dma_start(wo_s[:], wo.rearrange("(h d) n -> d h n", d=D)).then_inc(ld_late, 16)
            T["adj_free"].base = 0

            def body(t, graph, nxt, chunks):
                if graph:
                    for i in range(2):
                        sp.wait_ge(S["adj_free"], T["adj_free"].up())
                        sp.dma_start(adj_s[i], adj_v[:, 2 * t + 2 + i, :]).then_inc(adj_in[i], 16)
                sp.wait_ge(S["res_ready"], T["res_ready"].up())
                sp.dma_start(out_v[:, t, :], x1[:, t, :]).then_inc(out_done, 16)

            over_tiles(sp, T, body)
            sp.wait_ge(out_done, 16 * NT)

        @block.gpsimd
        def _(pool):
            T = tallies()
            nc.gpsimd.memset(k_t[:, 0:2].rearrange("p q h c -> p (q h c)"), 0.0).then_inc(pool_zero, 1)
            nc.gpsimd.memset(v[:, 0:NT // 2].rearrange("p t h d -> p (t h d)"), 0.0).then_inc(pool_zero, 1)

            def gather(h):
                pool.wait_ge(S["idx_ready"], T["idx_ready"].up())
                pool.nop(nofuse=True)
                for k in range(TOPK):
                    if k % 4 == 0:
                        pool.wait_ge(S["row_free"], T["row_free"].up())
                        pool.nop(nofuse=True)
                    nc.gpsimd.indirect_dma_start(
                        out=rows[:, k, :], out_offset=None, in_=kv,
                        in_offset=bass.IndirectOffsetOnAxis(ap=idx[:, h, k:k + 1], axis=0),
                    ).then_inc(row_in[k], 16)

            idx_t, row_t = T["idx_ready"], T["row_free"]
            row_t.base = 0
            with pool.Fori(0, NT) as t:
                idx_t.enter(t, 0, MH)
                row_t.enter(t, 0, 4 * MH)
                for h in range(MH):
                    gather(h)

        @block.scalar
        def _(act):
            T = tallies()
            T["pt_used"].base = T["sim_free"].base = 0
            act.dma_start(wqpk_s, wqpk).then_inc(ld_pk, 16)
            act.dma_start(keys_s, keys).then_inc(ld_pk, 16)
            act.dma_start(cst[:], const).then_inc(ld_c, 16)
            act.wait_ge(pro_dve, 1)
            nc.scalar.activation(stdx[:], mvx[:, :, 1], ACT.Sqrt, bias=small[:, 31:32]).then_inc(pro_act, 1)
            for b in range(4):
                act.wait_ge(pro_pe, b + 1)
                nc.scalar.activation(wcomb[:, b * BANK:(b + 1) * BANK], p_s[:, b * BANK:(b + 1) * BANK],
                                     ACT.Copy).then_inc(pro_act, 1)
            for b in range(4):
                act.wait_ge(pro_pe, 5 + b + 1)
                nc.scalar.activation(xn_t[:, b * BANK:(b + 1) * BANK], p_s[:, b * BANK:(b + 1) * BANK],
                                     ACT.Copy).then_inc(pro_act, 1)
            for b in range(4):
                act.wait_ge(pro_pe, 17 + b + 1)
                nc.scalar.activation(h_all[:, 4 * b:4 * b + 4, :],
                                     p_s[:, b * BANK:(b + 1) * BANK].rearrange("p (t d) -> p t d", t=4),
                                     ACT.Copy).then_inc(pro_act, 1)

            def take_c(out, in_, signal, scale=1.0):
                act.wait_ge(S["c_ready"], T["c_ready"].up())
                nc.scalar.activation(out, in_, ACT.Copy, scale=scale).then_inc(S["c_free_act"], 1)
                T["c_free_act"].up()
                act.wait_ge(S["c_free_act"], T["c_free_act"].now())
                act.sem_inc(S[signal], 1)
                T[signal].up()

            def take_x():
                n = T["x_free_act"].n
                act.wait_ge(S["x_ready"], T["x_ready"].up())
                act.wait_ge(S["pt_used"], T["pt_used"].up())
                nc.scalar.activation(pt[:, n % 2, :], p_x[:, T["x_ready"].n % 2 ^ 1, :],
                                     ACT.Copy).then_inc(S["x_free_act"], 1)
                T["x_free_act"].up()

            def graph_piece(p):
                T["x_ready"].up(4)
                act.wait_ge(S["u_ready"], T["u_ready"].up())
                nc.scalar.activation(u[p % 2], u[p % 2], ACT.Exp, bias=small[:, 8 + p % 2:9 + p % 2],
                                     accum_out=small[:, 10 + p % 2:11 + p % 2]).then_inc(S["gexp_ready"], 1)
                T["gexp_ready"].up()
                for _ in range(4):
                    take_x()
                T["c_ready"].up()

            def sqrt_step():
                act.wait_ge(S["var_ready"], T["var_ready"].up())
                nc.scalar.activation(std[:, 0:1], mv[:, 1:2], ACT.Sqrt, bias=small[:, 31:32]).then_inc(S["std_ready"], 1)
                T["std_ready"].up()

            def weights(h):
                act.wait_ge(S["top_ready"], T["top_ready"].up())
                nc.scalar.activation(wgt[:, h, :], top[:, h % 2, :], ACT.Exp, bias=small[:, 12 + h % 2:13 + h % 2],
                                     accum_out=small[:, 14 + h % 2:15 + h % 2]).then_inc(S["w_ready"], 1)
                T["w_ready"].up()

            def attend(h, chunks):
                act.wait_ge(S["max_ready"], T["max_ready"].up())
                nc.scalar.activation(prob[:, 0:chunks * BANK], p_s[:, 0:chunks * BANK], ACT.Exp,
                                     bias=small[:, 16 + h % 2:17 + h % 2],
                                     accum_out=small[:, 18 + h % 2:19 + h % 2]).then_inc(S["aexp_ready"], 1)
                T["aexp_ready"].up()
                for _ in range(chunks):
                    take_x()
                act.wait_ge(S["ot_ready"], T["ot_ready"].up())
                nc.scalar.activation(o_t[:], p_o[:, 0:P], ACT.Copy).then_inc(S["otc_ready"], 1)
                T["otc_ready"].up()

            def keys_values(t, h):
                act.wait_ge(S["acc_ready"], T["acc_ready"].up())
                nc.scalar.activation(v[:, t, h, :], acc[:, h % 2, D:2 * D], ACT.Copy).then_inc(S["kv_ready"], 1)
                act.wait_ge(S["c_ready"], T["c_ready"].up())
                quad, r = kpos(t)
                nc.scalar.activation(k_t[:, quad, h, bass.ds(r * P, P)], p_c[:, 0:P],
                                     ACT.Copy).then_inc(S["c_free_act"], 1)
                T["c_free_act"].up()
                act.wait_ge(S["c_free_act"], T["c_free_act"].now())
                act.sem_inc(S["kv_ready"], 1)
                T["kv_ready"].up(2)

            span_quad = [0]

            def kpos(t):
                return span_quad[0], t - 4 * span_quad[0]

            def front_start():
                sqrt_step()
                take_c(xn2_t[:], p_c[:, 0:P], "xn2t_ready")

            def take_sim(c):
                act.wait_ge(S["sim_free"], T["sim_free"].up())
                take_c(sim[:, c % 2].rearrange("p a b c -> p (a b c)"), p_c[:, :], "sim_ready")

            for p in range(GH):
                graph_piece(p)
            sqrt_step()
            front_start()
            for h in range(MH):
                if h % 2 == 0:
                    take_sim(h // 2)
                weights(h)
            for p in range(GH):
                graph_piece(p)
            sqrt_step()
            settle(T)

            def body(t, graph, nxt, chunks):
                span_quad[0] = chunks - 1
                for b in range(2):
                    take_c(q_t[:, 4 * b:4 * b + 4, :].rearrange("p a b -> p (a b)"), p_c[:, :], "qt_ready",
                           float(D) ** -0.5)
                if nxt:
                    front_start()
                for h in range(MH):
                    if nxt and h % 2 == 0:
                        take_sim(h // 2)
                    if graph:
                        graph_piece(h)
                    if h:
                        attend(h - 1, chunks)
                    keys_values(t, h)
                    if nxt:
                        weights(h)
                    if graph and h % GH == GH - 1:
                        sqrt_step()
                attend(MH - 1, chunks)

            over_tiles(act, T, body)

        @block.tensor
        def _(pe):
            T = tallies()
            pe.sem_inc(S["u_free"], 2)
            pe.sem_inc(S["pt_used"], 2)
            pe.wait_ge(ld_pk, 32)
            for b in range(4):
                for i in range(4 * b, 4 * b + 4):
                    last = nc.tensor.matmul(p_s[:, i * P:(i + 1) * P], wqpk_s[:, i * P:(i + 1) * P],
                                            keys_s[:, i * P:(i + 1) * P], start=True, stop=True)
                last.then_inc(pro_pe, 1)
            pe.wait_ge(ld_w, 48)
            last = nc.tensor.matmul(p_o[:, 0:8], wt_s, ab_s, start=True, stop=True)
            last.then_inc(pro_pe, 1)
            pe.wait_ge(pro_dve, 2)
            pe.wait_ge(ld_c, 16)
            for b in range(4):
                pe.wait_ge(pro_act, 1 + b + 1)
                for i in range(4 * b, 4 * b + 4):
                    last = nc.tensor.transpose(p_s[:, i * P:(i + 1) * P], xn[:, i * P:(i + 1) * P], ident)
                last.then_inc(pro_pe, 1)
            pe.wait_ge(pro_dve, 3)
            for s in range(2):
                for b in range(4):
                    if s == 0:
                        pe.wait_ge(pro_act, 5 + b + 1)
                    else:
                        pe.wait_ge(pro_dve, 3 + b + 1)
                    nc.tensor.matmul(p_s[:, b * BANK:(b + 1) * BANK], wrow[:, s, :], xn_t[:, b * BANK:(b + 1) * BANK],
                                     start=True, stop=True).then_inc(pro_pe, 1)
            for b in range(4):
                pe.wait_ge(pro_dve, 7 + b + 1)
                for i in range(4 * b, 4 * b + 4):
                    last = nc.tensor.matmul(p_s[:, i * P:(i + 1) * P], xn_t[:, i * P:(i + 1) * P], w_s,
                                            start=True, stop=True)
                last.then_inc(pro_pe, 1)
            pe.wait_ge(pro_act, 13)
            pe.wait_ge(ld_late, 64)
            pe.wait_ge(pool_zero, 2)

            taker_x = []
            taker_c = []

            def own_x(taker):
                if len(taker_x) >= 2:
                    who, value = taker_x[-2]
                    pe.wait_ge(S["x_free_" + who], value)
                bank = T["x_ready"].n % 2
                T["x_ready"].up()
                taker_x.append((taker, T["x_free_" + taker].up()))
                return p_x[:, bank, :]

            def own_c(taker):
                if taker_c:
                    pe.wait_ge(S["c_free_" + taker_c[-1]], T["c_free_" + taker_c[-1]].now())
                T["c_ready"].up()
                T["c_free_" + taker].up()
                taker_c.append(taker)
                return p_c

            def blocks(source, n_blocks, product):
                groups = n_blocks // 4
                def products(g):
                    n = T["pt_used"].n
                    pe.wait_ge(S["x_free_act"], mine[g][1])
                    for i in range(4):
                        last = product(4 * g + i, pt[:, n % 2, i * P:(i + 1) * P])
                    last.then_inc(S["pt_used"], 1)
                    T["pt_used"].up()
                    return last
                mine = []
                for g in range(groups):
                    bank = own_x("act")
                    mine.append(taker_x[-1])
                    for i in range(4):
                        last = nc.tensor.transpose(bank[:, i * P:(i + 1) * P],
                                                   source[:, (4 * g + i) * P:(4 * g + i + 1) * P], ident)
                    last.then_inc(S["x_ready"], 1)
                    if g:
                        products(g - 1)
                return products(groups - 1)

            def graph_logits(j):
                if j == 0:
                    pe.wait_ge(S["lt_ready"], T["lt_ready"].up())
                r = slice(32 * j, 32 * j + 32)
                for c in range(4):
                    bank = own_x("dve")
                    nc.tensor.matmul(bank, src_t[r, :], r_dst[r, c * BANK:(c + 1) * BANK],
                                     start=True, stop=True).then_inc(S["x_ready"], 1)

            def graph_out(p):
                j = p % GH
                pe.wait_ge(S["gexp_ready"], T["gexp_ready"].up())
                own_c("dve")
                last = blocks(u[p % 2], NT, lambda m, block_t: nc.tensor.matmul(
                    p_c[:, 0:GD], block_t, h_all[:, m, j * GD:(j + 1) * GD], start=(m == 0), stop=(m == NT - 1)))
                pe.wait_ge(S["pt_used"], T["pt_used"].now())
                pe.sem_inc(S["c_ready"], 1)
                pe.sem_inc(S["u_free"], 1)
                T["u_free"].up()

            def xn2_transpose():
                pe.wait_ge(S["xn2_ready"], T["xn2_ready"].up())
                own_c("act")
                nc.tensor.transpose(p_c[:, 0:P], xn2[:], ident).then_inc(S["c_ready"], 1)

            def similarity(c):
                if c == 0:
                    pe.wait_ge(S["xn2t_ready"], T["xn2t_ready"].up())
                own_c("act")
                nc.tensor.matmul(p_c[:], xn2_t[:], wcomb[:, c * BANK:(c + 1) * BANK],
                                 start=True, stop=True).then_inc(S["c_ready"], 1)

            def keys_transpose(h):
                pe.wait_ge(S["acc_ready"], T["acc_ready"].up())
                own_c("act")
                nc.tensor.transpose(p_c[:, 0:P], acc[:, h % 2, 0:D], ident).then_inc(S["c_ready"], 1)

            def scores(h, chunks):
                pe.wait_ge(S["kv_ready"], T["kv_ready"].up(2))
                if h == 0:
                    pe.wait_ge(S["qt_ready"], T["qt_ready"].up(2))
                for c in range(chunks):
                    last = nc.tensor.matmul(p_s[:, c * BANK:(c + 1) * BANK], q_t[:, h, :], k_t[:, c, h, :],
                                            start=True, stop=True)
                last.then_inc(S["s_ready"], 1)
                T["s_ready"].up()

            def attend(h, chunks):
                pe.wait_ge(S["aexp_ready"], T["aexp_ready"].up())
                pe.wait_ge(S["y_free"], T["y_free"].up())
                last = blocks(prob, 4 * chunks, lambda m, block_t: nc.tensor.matmul(
                    p_o[:, 0:P], v[:, m, h, :], block_t, start=(m == 0), stop=(m == 4 * chunks - 1)))
                pe.wait_ge(S["pt_used"], T["pt_used"].now())
                pe.sem_inc(S["ot_ready"], 1)
                T["ot_ready"].up()
                pe.wait_ge(S["otc_ready"], T["otc_ready"].up())
                nc.tensor.matmul(p_o[:, P:2 * P], o_t[:], wo_s[:, h, :], start=True, stop=True).then_inc(S["y_ready"], 1)
                T["y_ready"].up()

            T["y_free"].base = 0
            for p in range(GH):
                graph_logits(p)
                graph_out(p)
            xn2_transpose()
            for c in range(4):
                similarity(c)
            for p in range(GH):
                graph_logits(p)
                graph_out(p)
            settle(T)
            T["pt_used"].base += START["pt_used"]

            def body(t, graph, nxt, chunks):
                taker_x[:] = []
                pe.wait_ge(S["x_free_act"], T["x_free_act"].now())
                taker_c[:] = ["act"]
                pe.wait_ge(S["c_free_dve"], T["c_free_dve"].now())
                for b in range(2):
                    own_c("act")
                    for h in range(4 * b, 4 * b + 4):
                        last = nc.tensor.matmul(p_c[:, (h - 4 * b) * P:(h - 4 * b + 1) * P], wq_s[:, h * D:(h + 1) * D],
                                                xn2_t[:], start=True, stop=True)
                    last.then_inc(S["c_ready"], 1)
                if nxt:
                    xn2_transpose()
                for h in range(MH):
                    if nxt and h % 2 == 0:
                        similarity(h // 2)
                    if graph:
                        graph_logits(h % GH)
                        graph_out(h)
                    if h:
                        attend(h - 1, chunks)
                    keys_transpose(h)
                    scores(h, chunks)
                attend(MH - 1, chunks)

            over_tiles(pe, T, body)

        @block.vector
        def _(dve):
            T = tallies()
            T["u_free"].base = 0
            step = [0]

            def mark(ins):
                step[0] += 1
                ins.then_inc(dve_step, 1)

            def link(ins):
                step[0] += 1
                ins.then_inc(dve_step, 1)
                dve.wait_ge(dve_step, step[0])

            def restart():
                dve.sem_clear(dve_step)
                step[0] = 0

            dve.sem_inc(S["sim_free"], 2)
            dve.sem_inc(S["row_free"], 4)
            dve.sem_inc(S["kv_ready"], 4)
            dve.sem_inc(S["y_free"], 1)
            link(nc.vector.memset(small[:, 31:32], LN_EPS))
            link(nc.vector.memset(wrow[:, :, :], 0.0))
            dve.wait_ge(ld_x, 16)
            for m in range(NT):
                link(nc.vector.bn_stats(stat[:, 0:6], x1[:, m, :]))
                link(nc.vector.bn_aggr(mvx[:, m, :], stat[:, 0:6]))
            dve.sem_inc(pro_dve, 1)
            dve.wait_ge(pro_act, 1)
            link(nc.vector.reciprocal(stdx[:], stdx[:]))
            for m in range(NT):
                ins = nc.vector.tensor_scalar(xn[:, m * P:(m + 1) * P], x1[:, m, :], mvx[:, m, 0:1], stdx[:, m:m + 1],
                                              ALU.subtract, ALU.mult)
            ins.then_inc(pro_dve, 1)
            dve.wait_ge(pro_pe, 5)
            link(nc.vector.tensor_copy(wa_s, p_o[:, 0:8]))
            for s in range(2):
                for i in range(3):
                    ins = nc.vector.tensor_copy(
                        wrow[:, s, :].rearrange("p (j r) -> p j r", j=GH)[:, :, 3 * s + i],
                        wa_s[:, 4 * s:4 * s + 4])
            ins.then_inc(pro_dve, 1)
            dve.wait_ge(ld_c, 16)
            for s, (dest, cols) in enumerate(((r_src, src_cols), (r_dst, dst_cols))):
                for b in range(4):
                    dve.wait_ge(pro_pe, 9 + 4 * s + b + 1)
                    whole = p_s[:, b * BANK:(b + 1) * BANK]
                    link(nc.vector.tensor_copy(part, whole))
                    link(nc.vector.scalar_tensor_tensor(resid, part, cols[0], whole, ALU.mult, ALU.add))
                    link(nc.vector.tensor_copy(part, resid))
                    link(nc.vector.scalar_tensor_tensor(resid, part, cols[1], resid, ALU.mult, ALU.add))
                    nc.vector.tensor_scalar(dest[:, b * BANK:(b + 1) * BANK], resid, cols[2], None,
                                            ALU.add).then_inc(pro_dve, 1)
                    dve.wait_ge(pro_dve, 3 + 4 * s + b + 1)
            dve.wait_ge(ld_late, 64)

            def graph_start(i, g):
                link(nc.vector.tensor_copy(src_t, r_src[:, bass.ds(g * P, P)]))
                dve.sem_inc(S["lt_ready"], 1)
                T["lt_ready"].up()
                dve.wait_ge(adj_in[i], adj_wait[0])
                link(nc.vector.tensor_scalar(adj_s[i], adj_s[i], 0.0, MASKED, ALU.is_le, ALU.mult))

            def graph_piece(p, i):
                b = p % 2
                dve.wait_ge(S["u_free"], T["u_free"].up())
                for c in range(4):
                    bank = T["x_ready"].n % 2
                    dve.wait_ge(S["x_ready"], T["x_ready"].up())
                    dve.nop(nofuse=True)
                    nc.vector.tensor_tensor_reduce(
                        u[b][:, c * BANK:(c + 1) * BANK], adj_s[i][:, c * BANK:(c + 1) * BANK], p_x[:, bank, :],
                        1.0, LOWEST, ALU.add, ALU.max, small[:, c:c + 1]).then_inc(S["x_free_dve"], 1)
                    T["x_free_dve"].up()
                T["x_ready"].up(4)
                dve.wait_ge(S["x_free_dve"], T["x_free_dve"].now())
                link(nc.vector.tensor_reduce(small[:, 4:5], small[:, 0:4], AX_X, ALU.max))
                link(nc.vector.scalar_tensor_tensor(small[:, 5:6], small[:, 4:5], ALPHA, small[:, 4:5], ALU.mult, ALU.max))
                mark(nc.vector.tensor_scalar(small[:, 8 + b:9 + b], small[:, 5:6], -1.0, None, ALU.mult))
                link(nc.vector.scalar_tensor_tensor(u[b], u[b], ALPHA, u[b], ALU.mult, ALU.max))
                dve.sem_inc(S["u_ready"], 1)
                T["u_ready"].up()
                if p % GH == GH - 1:
                    dve.sem_inc(S["adj_free"], 1)
                    T["adj_free"].up()

            def graph_take(p):
                j, b = p % GH, p % 2
                dve.wait_ge(S["gexp_ready"], T["gexp_ready"].up())
                link(nc.vector.reciprocal(small[:, 20:21], small[:, 10 + b:11 + b]))
                dve.wait_ge(S["c_ready"], T["c_ready"].up())
                nc.vector.tensor_scalar(gout[:, j * GD:(j + 1) * GD], p_c[:, 0:GD], small[:, 20:21], None,
                                        ALU.mult).then_inc(S["c_free_dve"], 1)
                dve.wait_ge(S["c_free_dve"], T["c_free_dve"].up())

            def norm_stats(source):
                link(nc.vector.bn_stats(stat[:, 0:6], source))
                link(nc.vector.bn_aggr(mv[:], stat[:, 0:6]))
                dve.sem_inc(S["var_ready"], 1)
                T["var_ready"].up()

            def norm_apply(out, source):
                dve.wait_ge(S["std_ready"], T["std_ready"].up())
                link(nc.vector.reciprocal(std[:, 1:2], std[:, 0:1]))
                link(nc.vector.tensor_scalar(out, source, mv[:, 0:1], std[:, 1:2], ALU.subtract, ALU.mult))

            def graph_end(g):
                dve.wait_ge(S["c_free_dve"], T["c_free_dve"].now())
                norm_stats(gout[:])
                norm_apply(gout[:], gout[:])
                link(nc.vector.tensor_tensor(gout[:], gout[:], gam[:], ALU.mult))
                link(nc.vector.tensor_tensor(gout[:], gout[:], bet[:], ALU.add))
                link(nc.vector.tensor_tensor(x1[:, g, :], x1[:, g, :], gout[:], ALU.add))

            def front_start(t):
                norm_stats(x1[:, t, :])
                norm_apply(xn2[:], x1[:, t, :])
                dve.sem_inc(S["xn2_ready"], 1)
                T["xn2_ready"].up()

            def choose(h):
                if h % 2 == 0:
                    dve.wait_ge(S["sim_ready"], T["sim_ready"].up())
                dve.nop(nofuse=True)
                for half in range(2):
                    s = sim[:, (h // 2) % 2, h % 2, half, :]
                    link(nc.vector.max(best[:, half, 0:8], s))
                    mark(nc.vector.max_index(besti[:, half, 0:8], best[:, half, 0:8], s))
                    link(nc.vector.match_replace(rest[:], best[:, half, 0:8], s, LOWEST))
                    link(nc.vector.max(best[:, half, 8:16], rest[:]))
                    link(nc.vector.max_index(besti[:, half, 8:16], best[:, half, 8:16], rest[:]))
                if h % 2 == 1:
                    dve.sem_inc(S["sim_free"], 1)
                    T["sim_free"].up()
                mark(nc.vector.tensor_scalar(bestf[:, 0, :], besti[:, 0, :], 0.0, None, ALU.add))
                link(nc.vector.tensor_scalar(bestf[:, 1, :], besti[:, 1, :], float(NKEYS), float(h * NKEYS * NKEYS),
                                             ALU.mult, ALU.add))
                at = 0
                for i0, ni, nj in RECTS:
                    for dest, src in ((csum, best), (cidx, bestf)):
                        ins = nc.vector.tensor_tensor(
                            dest[:, at:at + ni * nj].rearrange("p (i j) -> p i j", i=ni),
                            src[:, 0, i0:i0 + ni].unsqueeze(2).to_broadcast([P, ni, nj]),
                            src[:, 1, 0:nj].unsqueeze(1).to_broadcast([P, ni, nj]), ALU.add)
                        mark(ins)
                    at += ni * nj
                dve.wait_ge(dve_step, step[0])
                b = h % 2
                link(nc.vector.max(top[:, b, 0:8], csum[:]))
                mark(nc.vector.max_index(pos[:, 0:8], top[:, b, 0:8], csum[:]))
                mark(nc.vector.tensor_scalar(small[:, 12 + b:13 + b], top[:, b, 0:1], -1.0, None, ALU.mult))
                link(nc.vector.match_replace(crest[:], top[:, b, 0:8], csum[:], LOWEST))
                link(nc.vector.max(top[:, b, 8:16], crest[:]))
                dve.sem_inc(S["top_ready"], 1)
                T["top_ready"].up()
                link(nc.vector.max_index(pos[:, 8:16], top[:, b, 8:16], crest[:]))
                link(nc.vector.tensor_copy(posf[:], pos[:]))
                link(nc.vector.tensor_tensor(hot[:], posf[:].unsqueeze(2).to_broadcast([P, TOPK, NC]),
                                             iota.unsqueeze(1).to_broadcast([P, TOPK, NC]), ALU.is_equal))
                link(nc.vector.tensor_tensor(hot[:], hot[:], cidx[:].unsqueeze(1).to_broadcast([P, TOPK, NC]), ALU.mult))
                link(nc.vector.tensor_reduce(idxf[:], hot[:], AX_X, ALU.add))
                link(nc.vector.tensor_copy(idx[:, h, :], idxf[:]))
                dve.sem_inc(S["idx_ready"], 1)
                T["idx_ready"].up()

            def weights(h):
                b = h % 2
                dve.wait_ge(S["w_ready"], T["w_ready"].up())
                link(nc.vector.reciprocal(small[:, 21:22], small[:, 14 + b:15 + b]))
                link(nc.vector.tensor_scalar(wgt[:, h, :], wgt[:, h, :], small[:, 21:22], None, ALU.mult))

            def combine(t, h):
                b = h % 2
                dve.wait_ge(S["kv_ready"], T["kv_ready"].up(2) - 4)
                for k in range(TOPK):
                    dve.wait_ge(row_in[k], (t * MH + h + 1) * 16)
                    if k == 0:
                        ins = nc.vector.tensor_scalar(acc[:, b, :], rows[:, 0, :], wgt[:, h, 0:1], None, ALU.mult)
                    else:
                        ins = nc.vector.scalar_tensor_tensor(acc[:, b, :], rows[:, k, :], wgt[:, h, k:k + 1],
                                                             acc[:, b, :], ALU.mult, ALU.add)
                    link(ins)
                    if k % 4 == 3:
                        dve.sem_inc(S["row_free"], 1)
                        T["row_free"].up()
                dve.sem_inc(S["acc_ready"], 1)
                T["acc_ready"].up()

            def row_max(h, chunks):
                b = h % 2
                dve.wait_ge(S["s_ready"], T["s_ready"].up())
                dve.nop(nofuse=True)
                last = p_s[:, (chunks - 1) * BANK:chunks * BANK]
                link(nc.vector.tensor_tensor_reduce(last, last, cmask[:], 1.0, LOWEST, ALU.add, ALU.max, small[:, 24:25]))
                if chunks > 1:
                    link(nc.vector.tensor_reduce(small[:, 25:26], p_s[:, 0:(chunks - 1) * BANK], AX_X, ALU.max))
                    link(nc.vector.tensor_tensor(small[:, 24:25], small[:, 24:25], small[:, 25:26], ALU.max))
                link(nc.vector.tensor_scalar(small[:, 16 + b:17 + b], small[:, 24:25], -1.0, None, ALU.mult))
                dve.sem_inc(S["max_ready"], 1)
                T["max_ready"].up()

            def add_head(t, h):
                b = h % 2
                dve.wait_ge(S["aexp_ready"], T["aexp_ready"].up())
                link(nc.vector.reciprocal(small[:, 26:27], small[:, 18 + b:19 + b]))
                dve.wait_ge(S["y_ready"], T["y_ready"].up())
                nc.vector.scalar_tensor_tensor(x1[:, t, :], p_o[:, P:2 * P], small[:, 26:27], x1[:, t, :],
                                               ALU.mult, ALU.add).then_inc(S["y_free"], 1)
                dve.wait_ge(S["y_free"], T["y_free"].up())

            adj_wait = [16]
            graph_start(0, 0)
            for p in range(GH):
                graph_piece(p, 0)
                if p:
                    graph_take(p - 1)
            graph_take(GH - 1)
            graph_end(0)
            front_start(0)
            for h in range(MH):
                choose(h)
                weights(h)
            T["c_ready"].up(5)
            graph_start(1, 1)
            for p in range(GH):
                graph_piece(p, 1)
                if p:
                    graph_take(p - 1)
            graph_take(GH - 1)
            graph_end(1)
            settle(T)
            restart()

            def body(t, graph, nxt, chunks):
                quad = chunks - 1
                adj_wait[0] = (t + 2) * 16
                T["c_ready"].up(2)
                link(nc.vector.tensor_copy(cmask[:], cst[:, bass.ds((t - 4 * quad) * (-P) + (C_CAUSAL + 3 * P), BANK)]))
                if nxt:
                    front_start(t + 1)
                    T["c_ready"].up()
                for h in range(MH):
                    if nxt and h % 2 == 0:
                        T["c_ready"].up()
                    if graph:
                        if h % GH == 0:
                            graph_start(h // GH, 2 * t + 2 + h // GH)
                        graph_piece(h, h // GH)
                    elif isinstance(t, int) and t == NT // 2 - 1:
                        link(nc.vector.memset(k_t[:, 2:4, h, :], 0.0))
                        link(nc.vector.memset(v[:, NT // 2 + h, :, :], 0.0))
                    if h:
                        T["x_ready"].up(chunks)
                        row_max(h - 1, chunks)
                    combine(t, h)
                    if graph:
                        graph_take(h)
                    T["c_ready"].up()
                    if nxt:
                        choose(h)
                        weights(h)
                    if h:
                        add_head(t, h - 1)
                    if graph and h % GH == GH - 1:
                        graph_end(2 * t + 2 + h // GH)
                T["x_ready"].up(chunks)
                row_max(MH - 1, chunks)
                add_head(t, MH - 1)
                dve.sem_inc(S["res_ready"], 1)
                restart()

            over_tiles(dve, T, body)


def settle(T):
    fixed = dict(x_ready=64, x_free_dve=32, x_free_act=32, c_ready=13, c_free_act=5, c_free_dve=8, pt_used=32,
                 u_free=8, u_ready=8, gexp_ready=8, lt_ready=2, adj_free=2, s_ready=0, max_ready=0, aexp_ready=0,
                 acc_ready=0, kv_ready=4, ot_ready=0, otc_ready=0, y_ready=0, top_ready=8, w_ready=8, idx_ready=8,
                 sim_ready=4, sim_free=4, var_ready=3, std_ready=3, xn2_ready=1, xn2t_ready=1, qt_ready=0,
                 res_ready=0)
    for n, value in fixed.items():
        T[n].base, T[n].n = value, 0


def constants(np):
    c = np.zeros((P, C_END), np.float32)
    c[:, C_IDENT:C_IDENT + P] = np.eye(P)
    col = np.arange(BANK + 3 * P)[None, :] - 3 * P
    c[:, C_CAUSAL:C_IOTA] = np.where(col <= np.arange(P)[:, None], 0.0, -3.0e38)
    c[:, C_IOTA:C_THIRDS] = np.arange(NC)
    r = np.arange(P) % 32
    for s in range(2):
        third = r - 3 * s
        c[:, C_THIRDS + 3 * s] = -1.0 * ((third == 1) | (third == 2))
        c[:, C_THIRDS + 3 * s + 1] = -1.0 * (third == 2)
        c[:, C_THIRDS + 3 * s + 2] = (r < 6) & ((third < 0) | (third > 2))
    return c


def kernel(**inputs):
    import numpy as np
    import concourse.bacc as _bacc
    from concourse.bass_utils import run_bass_kernel_spmd as _run

    f = {n: np.asarray(a) for n, a in inputs.items()}
    a = f["L0_gnn_a"]
    a_blk = np.zeros((P, 2 * GH), a.dtype)
    for j in range(GH):
        a_blk[j * GD:(j + 1) * GD, j] = a[0:GD, 0]
        a_blk[j * GD:(j + 1) * GD, GH + j] = a[GD:2 * GD, 0]
    arrays = dict(
        x=f["x"], adj=f["adj"], w=f["L0_gnn_W"], w_t=f["L0_gnn_W"].T, a_blk=a_blk,
        gamma=f["L0_gnn_gamma"], beta=f["L0_gnn_beta"],
        wqpk=f["L0_ffn_Wq_pk"].reshape(D, 2, MH, DKEY).transpose(3, 2, 1, 0).reshape(DKEY, N),
        keys=f["L0_ffn_pk_keys"].transpose(3, 2, 0, 1).reshape(DKEY, N),
        wq=f["L0_ffn_Wq"],
        kv=np.concatenate([f["L0_ffn_keys_table"], f["L0_ffn_values_table"]], axis=1),
        wo=f["L0_ffn_Wo"], const=constants(np),
    )
    arrays = {n: np.ascontiguousarray(v) for n, v in arrays.items()}
    nc = _bacc.Bacc("TRN2", target_bir_lowering=False, num_devices=1)
    args = [nc.dram_tensor(n, v.shape, mybir.dt.from_np(v.dtype), kind="ExternalInput").ap()
            for n, v in arrays.items()]
    args.append(nc.dram_tensor("out", (N, D), F32, kind="ExternalOutput").ap())
    build(nc, *args)
    r = _run(nc, [arrays], core_ids=[0])
    return r.results[0]["out"]
```

```python
from contextlib import ExitStack

import concourse.bass as bass
from concourse import mybir

F32 = mybir.dt.float32
BF16 = mybir.dt.bfloat16
U32 = mybir.dt.uint32
U16 = mybir.dt.uint16
ALU = mybir.AluOpType
ACT = mybir.ActivationFunctionType
AX_X = mybir.AxisListType.X

P = 128
N = 2048
NT = N // P
D = 128
GH, GD = 4, 32
MH = 8
NKEYS = 128
DKEY = 64
TOPK = 16
BANK = 512
ALPHA = 0.2
LN_EPS = 1e-5
MASKED = -9.0e15
LOWEST = -3.0e38
RECTS = [(0, 1, 16), (1, 1, 8), (2, 2, 5), (4, 4, 3), (8, 8, 1)]
NC = sum(a * b for _, a, b in RECTS)
SPANS = [(0, 1, 8, 1), (1, 4, 8, 1), (4, 5, 8, 1), (5, 6, 8, 1), (6, 7, 8, 1), (7, 8, 4, 1), (8, 9, 0, 1), (9, 12, 0, 1),
         (12, 13, 0, 1), (13, 15, 0, 1), (15, 16, 0, 0)]
C_IDENT, C_THIRDS, C_HEADS, C_END = 0, P, P + 6, P + 6 + GH
CB_END = P + BANK + 3 * P


class Tally:

    def __init__(self, start=0):
        self.base, self.n, self.t, self.first, self.per = start, 0, None, 0, 0

    def enter(self, t, first, per):
        self.t, self.first, self.per = t, first, per

    def leave(self, bodies):
        assert self.n in (0, self.per), (self.n, self.per)
        self.base += self.per * bodies
        self.n, self.t = 0, None

    def up(self, k=1):
        self.n += k
        return self.now()

    def now(self):
        if self.t is None:
            return self.base + self.n
        if isinstance(self.t, int):
            return self.base + self.n + (self.t - self.first) * self.per
        return self.t * self.per + (self.base + self.n - self.first * self.per)


def per_body(first, pieces, nxt):
    outs = pieces + int(0 < first < NT // 2) - (pieces == MH)
    stored = MH - (first == 0)
    chunks = sum(((first + (h - 2) // MH) // 4 + 1) for h in range(MH) if first or h > 1)
    sims = 2 + 2 * nxt
    c = outs + stored + 2 + sims + nxt
    norms = int(0 < first < NT // 2) + (pieces > 0) + nxt
    return dict(x=4 * outs + chunks, c=c, norm=norms)


PROLOGUE = dict(x=4 * GH, c=GH + 3, norm=2)
BUFFERS = 2
RING_PARTS = 4


def build(nc, x, adj, w, w_t, a_blk, gamma, beta, wqpk, keys, wq, kv, wo, const, const_bf, iota16, out):
    with ExitStack() as ctx:
        def sb(name, shape, dt=F32):
            return ctx.enter_context(nc.sbuf_tensor(name, shape, dt))

        def ps(name, shape):
            return ctx.enter_context(nc.psum_tensor(name, shape, F32))

        def sem(name):
            return ctx.enter_context(nc.semaphore(name))

        k_t = sb("k_t", [P, 4, MH, BANK])
        v = sb("v", [P, NT, MH, D])
        rows = sb("rows", [P, TOPK, 2 * D])
        wcomb = sb("wcomb", [P, MH * 2 * NKEYS])
        wq_s = sb("wq_s", [P, MH * D])
        wo_s = sb("wo_s", [P, MH, D])
        x1 = sb("x1", [P, NT, D])
        prob = sb("prob", [P, N])
        pt = sb("pt", [P, 2, BANK])
        sim = sb("sim", [P, 2, 2, 2, NKEYS])
        q_t = sb("q_t", [P, MH, P])
        cst = sb("cst", [P, C_END])
        cstb = sb("cstb", [P, CB_END], BF16)
        iota = sb("iota", [P, TOPK, NC], U16)
        gam = sb("gam", [P, D])
        bet = sb("bet", [P, D])
        acc = sb("acc", [P, 2, 2 * D])
        acc_odd = sb("acc_odd", [P, 2 * D])
        o_t = sb("o_t", [P, P])
        xn2 = sb("xn2", [P, D])
        xn2_t = sb("xn2_t", [P, P])
        gout = sb("gout", [P, GH, GD])
        best = sb("best", [P, 2, 2, TOPK])
        besti = sb("besti", [P, 2, TOPK], U32)
        rest = sb("rest", [P, 2, NKEYS])
        pair = sb("pair", [P, 2, NC])
        prest = sb("prest", [P, NC])
        top = sb("top", [P, 2, TOPK])
        pos = sb("pos", [P, TOPK], U32)
        posx = sb("posx", [P, TOPK, NC], U16)
        pidx = sb("pidx", [P, NC], U16)
        hot = sb("hot", [P, TOPK, NC], U16)
        idx = sb("idx", [P, MH, TOPK], U32)
        wgt = sb("wgt", [P, MH, TOPK])
        stat = sb("stat", [P, 6])
        mv = sb("mv", [P, 2])
        std = sb("std", [P, 2])
        eps = sb("eps", [P, 1])
        umax = sb("umax", [P, 4])
        neg_umax = sb("neg_umax", [P, 2])
        gsum = sb("gsum", [P, 2, GH])
        grec = sb("grec", [P, GH])
        neg_top = sb("neg_top", [P, 2])
        wsum = sb("wsum", [P, 2])
        wrec = sb("wrec", [P, 2])
        neg_max = sb("neg_max", [P, 2])
        psum_row = sb("psum_row", [P, 2])
        prec = sb("prec", [P, 1])
        mvx = sb("mvx", [P, NT, 2])
        stdx = sb("stdx", [P, NT])
        k_hi = k_t[:, 2:4].rearrange("p q h c -> p (q h c)")
        v_hi = v[:, NT // 2:NT].rearrange("p t h d -> p (t h d)")
        xn_t = k_hi[:, 0:N]
        h_all = k_hi[:, N:2 * N].rearrange("p (t d) -> p t d", t=NT)
        r_src = k_hi[:, 2 * N:2 * N + N // 2].bitcast(BF16)
        r_dst = k_hi[:, 2 * N + N // 2:3 * N].bitcast(BF16)
        spare = k_hi[:, 3 * N:4 * N]
        wrow = spare[:, 0:2 * P].rearrange("p (a b) -> p a b", a=2)
        src_t = spare[:, 2 * P:4 * P].bitcast(BF16).rearrange("p (j n) -> p j n", j=GH)
        w_s = spare[:, 4 * P:5 * P]
        ab_s = spare[:, 5 * P:5 * P + 8]
        wa_s = spare[:, 5 * P + 8:5 * P + 16]
        part = spare[:, 6 * P:8 * P].bitcast(BF16)
        relu = spare[:, 8 * P:16 * P].rearrange("p (a b) -> p a b", a=2)
        wt_s = spare[:, 8 * P:9 * P]
        u = [v_hi[:, 0:N], v_hi[:, N:2 * N]]
        adj_s = v_hi[:, 2 * N:3 * N]
        mask = [v_hi[:, 3 * N:3 * N + N // 2].bitcast(BF16), v_hi[:, 3 * N + N // 2:4 * N].bitcast(BF16)]
        wqpk_s = v_hi[0:DKEY, 0:N]
        keys_s = v_hi[0:DKEY, N:2 * N]
        xn = prob
        resid = pt[:, 0, :]
        cstb_f32 = sim[:].rearrange("p a b c d -> p (a b c d)")

        ident = cst[:, C_IDENT:C_IDENT + P]
        ident_bf = cstb[:, 0:P]
        head_cols = [cst[:, C_HEADS + j:C_HEADS + j + 1] for j in range(GH)]
        src_cols = [cst[:, C_THIRDS + i:C_THIRDS + i + 1] for i in range(3)]
        dst_cols = [cst[:, C_THIRDS + i:C_THIRDS + i + 1] for i in range(3, 6)]

        p_s = ps("p_s", [P, 4 * BANK])
        p_l = [p_s[:, (2 + i) * BANK:(3 + i) * BANK] for i in range(2)]
        p_x = ps("p_x", [P, 2, BANK])
        p_c = ps("p_c", [P, BANK])
        p_o = ps("p_o", [P, BANK])

        names = list(PROLOGUE)
        adj_free, mask_ready = sem("adj_free"), sem("mask_ready")
        l_ready, relu_ready, l_free = sem("l_ready"), sem("relu_ready"), sem("l_free")
        u_ready, gexp_ready, u_free, gout_ready = sem("u_ready"), sem("gexp_ready"), sem("u_free"), sem("gout_ready")
        var_ready, std_ready, xn2_ready = sem("var_ready"), sem("std_ready"), sem("xn2_ready")
        sim_ready, sim_free, top_ready, pos_ready = sem("sim_ready"), sem("sim_free"), sem("top_ready"), sem("pos_ready")
        wsum_ready, w_ready, idx_ready, row_free = sem("wsum_ready"), sem("w_ready"), sem("idx_ready"), sem("row_free")
        acc_ready, kv_ready, s_ready, max_ready = sem("acc_ready"), sem("kv_ready"), sem("s_ready"), sem("max_ready")
        aexp_ready, ot_ready, otc_ready = sem("aexp_ready"), sem("ot_ready"), sem("otc_ready")
        y_ready, y_free, res_ready = sem("y_ready"), sem("y_free"), sem("res_ready")
        x_ready, x_free, pt_used, c_ready, c_free = sem("x_ready"), sem("x_free"), sem("pt_used"), sem("c_ready"), sem("c_free")
        row_in = [sem(f"row_in{k}") for k in range(TOPK)]
        adj_in = sem("adj_in")
        ld_x, ld_w, ld_pk, ld_c, ld_late = sem("ld_x"), sem("ld_w"), sem("ld_pk"), sem("ld_c"), sem("ld_late")
        out_done = sem("out_done")
        pool_zero = sem("pool_zero")
        dve_step = sem("dve_step")
        pro_pe, pro_act, pro_dve = sem("pro_pe"), sem("pro_act"), sem("pro_dve")

        x_v = x.rearrange("(t p) d -> p t d", p=P)
        out_v = out.rearrange("(t p) d -> p t d", p=P)
        adj_v = adj.rearrange("(t p) m -> p t m", p=P)

        def tallies():
            return {n: Tally() for n in names}

        def settle(T):
            for n in names:
                assert T[n].n in (0, PROLOGUE[n]), (n, T[n].n)
                T[n].base, T[n].n = PROLOGUE[n], 0

        def over_tiles(eng, T, body):
            for first, end, pieces, nxt in SPANS:
                per = per_body(first, pieces, nxt)

                def one(t):
                    for n in names:
                        T[n].enter(t, first, per[n])
                    body(t, first, pieces, nxt)

                if end - first == 1:
                    one(first)
                else:
                    with eng.Fori(first, end) as t:
                        one(t)
                for n in names:
                    T[n].leave(end - first)

        def chunks_of(first, h):
            return (first - (h < 0)) // 4 + 1

        def nth(t, h, parts=1, k=0):
            return t * (MH * parts) + (h * parts + k + 1)

        block = ctx.enter_context(nc.Block())

        @block.sync
        def _(sp):
            T = tallies()
            sp.dma_start(x1[:], x_v).then_inc(ld_x, 16)
            sp.dma_start(wt_s, w_t).then_inc(ld_w, 16)
            sp.dma_start(ab_s, a_blk).then_inc(ld_w, 16)
            sp.dma_start(w_s, w).then_inc(ld_w, 16)
            sp.dma_start(adj_s, adj_v[:, 0, :]).then_inc(adj_in, 16)
            sp.dma_start(wq_s[:], wq).then_inc(ld_late, 16)
            sp.dma_start(wo_s[:], wo.rearrange("(h d) n -> d h n", d=D)).then_inc(ld_late, 16)
            sp.dma_start(gam[:], gamma.partition_broadcast(P)).then_inc(ld_late, 16)
            sp.dma_start(bet[:], beta.partition_broadcast(P)).then_inc(ld_late, 16)

            for g in range(1, 3):
                sp.wait_ge(adj_free, g)
                sp.dma_start(adj_s, adj_v[:, g, :]).then_inc(adj_in, 16)

            def body(t, first, pieces, nxt):
                if first:
                    sp.wait_ge(res_ready, t)
                    sp.dma_start(out_v[:, t - 1, :], x1[:, t - 1, :]).then_inc(out_done, 16)
                if pieces == MH:
                    for g in range(3, 5):
                        if first == 6 and g == 4:
                            continue
                        sp.wait_ge(adj_free, 2 * t + g)
                        sp.dma_start(adj_s, adj_v[:, 2 * t + g, :]).then_inc(adj_in, 16)

            over_tiles(sp, T, body)
            sp.wait_ge(res_ready, NT)
            sp.dma_start(out_v[:, NT - 1, :], x1[:, NT - 1, :]).then_inc(out_done, 16)
            sp.wait_ge(out_done, 16 * NT)

        @block.gpsimd
        def _(pool):
            nc.gpsimd.memset(k_t[:, 0:2].rearrange("p q h c -> p (q h c)"), 0.0).then_inc(pool_zero, 1)
            nc.gpsimd.memset(v[:, 0:NT // 2].rearrange("p t h d -> p (t h d)"), 0.0).then_inc(pool_zero, 1)
            with pool.Fori(0, NT) as t:
                for h in range(MH):
                    pool.wait_ge(idx_ready, nth(t, h))
                    pool.nop(nofuse=True)
                    for k in range(TOPK):
                        if k % 4 == 0:
                            pool.wait_ge(row_free, nth(t, h, RING_PARTS, k // 4))
                            pool.nop(nofuse=True)
                        nc.gpsimd.indirect_dma_start(
                            out=rows[:, k, :], out_offset=None, in_=kv,
                            in_offset=bass.IndirectOffsetOnAxis(ap=idx[:, h, k:k + 1], axis=0),
                        ).then_inc(row_in[k], 16)

        @block.scalar
        def _(act):
            T = tallies()
            act.dma_start(wqpk_s, wqpk).then_inc(ld_pk, 16)
            act.dma_start(keys_s, keys).then_inc(ld_pk, 16)
            act.dma_start(cst[:], const).then_inc(ld_c, 16)
            act.dma_start(cstb_f32, const_bf).then_inc(ld_c, 16)
            act.dma_start(iota[:].rearrange("p a b -> p (a b)"), iota16).then_inc(ld_c, 16)
            for b in range(4):
                act.wait_ge(pro_pe, b + 1)
                nc.scalar.activation(wcomb[:, b * BANK:(b + 1) * BANK], p_s[:, b * BANK:(b + 1) * BANK],
                                     ACT.Copy).then_inc(pro_act, 1)
            act.wait_ge(ld_c, 48)
            nc.scalar.activation(cstb[:], cstb_f32, ACT.Copy).then_inc(pro_act, 1)
            act.wait_ge(pro_dve, 1)
            nc.scalar.activation(stdx[:], mvx[:, :, 1], ACT.Sqrt, bias=eps[:]).then_inc(pro_act, 1)
            for b in range(4):
                act.wait_ge(pro_pe, 5 + b + 1)
                nc.scalar.activation(xn_t[:, b * BANK:(b + 1) * BANK], p_s[:, b * BANK:(b + 1) * BANK],
                                     ACT.Copy).then_inc(pro_act, 1)
            for b in range(4):
                act.wait_ge(pro_pe, 17 + b + 1)
                nc.scalar.activation(h_all[:, 4 * b:4 * b + 4, :],
                                     p_s[:, b * BANK:(b + 1) * BANK].rearrange("p (t d) -> p t d", t=4),
                                     ACT.Copy).then_inc(pro_act, 1)

            def take_c(out, in_, scale=1.0):
                act.wait_ge(c_ready, T["c"].up())
                nc.scalar.activation(out, in_, ACT.Copy, scale=scale).then_inc(c_free, 1)

            def tell(semaphore):
                act.wait_ge(c_free, T["c"].now())
                act.sem_inc(semaphore, 1)

            def take_x():
                n = T["x"].n
                act.wait_ge(x_ready, T["x"].up())
                act.wait_ge(pt_used, T["x"].now() + (BUFFERS - 2))
                nc.scalar.activation(pt[:, n % 2, :], p_x[:, n % 2, :], ACT.Copy).then_inc(x_free, 1)

            def graph_relu(t, p, chunks):
                for c in chunks:
                    act.wait_ge(l_ready, nth(t, GH + p, 4, c))
                    nc.scalar.activation(relu[:, c % 2, :], p_l[c % 2], ACT.Relu,
                                         scale=1.0 / ALPHA - 1.0).then_inc(relu_ready, 1)

            def graph_exp(t, p):
                b, j = p % 2, p % GH
                par = 1 if t is None else p // GH
                act.wait_ge(u_ready, nth(0, p) if t is None else nth(t, GH + p))
                nc.scalar.activation(u[b], u[b], ACT.Exp, bias=neg_umax[:, b:b + 1],
                                     accum_out=gsum[:, par, j:j + 1]).then_inc(gexp_ready, 1)

            def graph_take(p):
                take_c(gout[:, p % GH, :], p_c[:, 0:GD])
                tell(gout_ready)

            def sqrt_step():
                act.wait_ge(var_ready, T["norm"].up())
                nc.scalar.activation(std[:, 0:1], mv[:, 1:2], ACT.Sqrt, bias=eps[:]).then_inc(std_ready, 1)

            def choice_copies(t, h):
                b, w = h % 2, h % MH
                act.wait_ge(top_ready, nth(t, h))
                nc.scalar.activation(posx[:], pos[:].unsqueeze(2).to_broadcast([P, TOPK, NC]), ACT.Copy)
                nc.scalar.activation(pidx[:], pair[:, 1, :], ACT.Copy).then_inc(pos_ready, 1)
                nc.scalar.activation(wgt[:, w, :], top[:, b, :], ACT.Exp, bias=neg_top[:, b:b + 1],
                                     accum_out=wsum[:, b:b + 1]).then_inc(wsum_ready, 1)

            def weights(t, h):
                b, w = h % 2, h % MH
                act.wait_ge(idx_ready, nth(t, h))
                nc.scalar.activation(wgt[:, w, :], wgt[:, w, :], ACT.Copy, scale=wrec[:, b:b + 1]).then_inc(w_ready, 1)

            def attend_exp(t, h, chunks):
                b = h % 2
                act.wait_ge(max_ready, nth(t, h))
                nc.scalar.activation(prob[:, 0:chunks * BANK], p_s[:, 0:chunks * BANK], ACT.Exp,
                                     bias=neg_max[:, b:b + 1], accum_out=psum_row[:, b:b + 1]).then_inc(aexp_ready, 1)

            def attend_copies(t, h, chunks):
                for _ in range(chunks):
                    take_x()
                act.wait_ge(ot_ready, nth(t, h))
                nc.scalar.activation(o_t[:], p_o[:, 0:P], ACT.Copy).then_inc(otc_ready, 1)

            def store_kv(t, h, quad):
                tile = t - (h < 0)
                take_c(k_t[:, quad, h % MH, bass.ds((tile - 4 * quad) * P, P)], p_c[:, 0:P])
                act.wait_ge(acc_ready, nth(t, h))
                nc.scalar.activation(v[:, tile, h % MH, :], acc[:, h % 2, D:2 * D], ACT.Copy).then_inc(kv_ready, 1)

            def take_sim(t, c):
                act.wait_ge(sim_free, t * (MH // 2) + (c + 1))
                take_c(sim[:, c % 2].rearrange("p a b c -> p (a b c)"), p_c[:, :])
                tell(sim_ready)

            graph_relu(0, -GH, range(4))
            for p in range(GH):
                graph_exp(None, p)
                graph_relu(0, p + 1 - GH, range(4) if p < GH - 1 else range(2))
                for _ in range(4):
                    take_x()
                graph_take(p)
            sqrt_step()
            sqrt_step()
            take_c(xn2_t[:], p_c[:, 0:P])
            for c in range(2):
                take_sim(0, c)
            for h in range(2):
                choice_copies(0, h)
                weights(0, h)
            settle(T)

            def body(t, first, pieces, nxt):
                ended = 0 < first < NT // 2
                for h in range(MH):
                    out_now = h - 1 < pieces if h else ended
                    norm_now = (h == 0 and ended) or (h == GH and pieces)
                    choose = h < 6 or nxt
                    if out_now:
                        take_x()
                        take_x()
                    if first or h > 1:
                        attend_exp(t, h - 2, chunks_of(first, h - 2))
                    if h < pieces:
                        graph_relu(t, h, (2, 3))
                    if out_now:
                        take_x()
                        take_x()
                        graph_take(h - 1)
                    if h == 5 and nxt:
                        sqrt_step()
                    if first or h > 0:
                        store_kv(t, h - 1, chunks_of(first, h - 1) - 1)
                    if choose:
                        choice_copies(t, h + 2)
                    if first or h > 1:
                        attend_copies(t, h - 2, chunks_of(first, h - 2))
                    if norm_now:
                        sqrt_step()
                    if h < pieces:
                        graph_exp(t, h)
                    if choose:
                        weights(t, h + 2)
                    if h == 0:
                        for b in range(2):
                            take_c(q_t[:, 4 * b:4 * b + 4, :].rearrange("p a b -> p (a b)"), p_c[:, :],
                                   scale=float(D) ** -0.5)
                    if h == 5 and nxt:
                        take_c(xn2_t[:], p_c[:, 0:P])
                    if h % 2 and (h < 4 or nxt):
                        take_sim(t, (h + 3) // 2)
                    if h + 1 < pieces or pieces == MH:
                        graph_relu(t, h + 1, (0, 1))

            over_tiles(act, T, body)
            attend_exp(NT, -2, NT // 4)
            store_kv(NT, -1, NT // 4 - 1)
            attend_copies(NT, -2, NT // 4)
            attend_exp(NT, -1, NT // 4)
            attend_copies(NT, -1, NT // 4)

        @block.tensor
        def _(pe):
            T = tallies()
            pe.sem_inc(u_free, BUFFERS)
            pe.sem_inc(pt_used, BUFFERS)
            pe.wait_ge(ld_pk, 32)
            for b in range(4):
                for i in range(4 * b, 4 * b + 4):
                    last = nc.tensor.matmul(p_s[:, i * P:(i + 1) * P], wqpk_s[:, i * P:(i + 1) * P],
                                            keys_s[:, i * P:(i + 1) * P], start=True, stop=True)
                last.then_inc(pro_pe, 1)
            pe.wait_ge(ld_w, 48)
            nc.tensor.matmul(p_o[:, 0:8], wt_s, ab_s, start=True, stop=True).then_inc(pro_pe, 1)
            pe.wait_ge(pro_dve, 2)
            pe.wait_ge(ld_c, 48)
            for b in range(4):
                pe.wait_ge(pro_act, b + 1)
                for i in range(4 * b, 4 * b + 4):
                    last = nc.tensor.transpose(p_s[:, i * P:(i + 1) * P], xn[:, i * P:(i + 1) * P], ident)
                last.then_inc(pro_pe, 1)
            pe.wait_ge(pro_dve, 3)
            for s in range(2):
                for b in range(4):
                    if s == 0:
                        pe.wait_ge(pro_act, 6 + b + 1)
                    else:
                        pe.wait_ge(pro_dve, 3 + b + 1)
                    nc.tensor.matmul(p_s[:, b * BANK:(b + 1) * BANK], wrow[:, s, :], xn_t[:, b * BANK:(b + 1) * BANK],
                                     start=True, stop=True).then_inc(pro_pe, 1)
            for b in range(4):
                pe.wait_ge(pro_dve, 7 + b + 1)
                for i in range(4 * b, 4 * b + 4):
                    last = nc.tensor.matmul(p_s[:, i * P:(i + 1) * P], xn_t[:, i * P:(i + 1) * P], w_s,
                                            start=True, stop=True)
                last.then_inc(pro_pe, 1)
            pe.wait_ge(pro_act, 14)

            def own_x():
                n = T["x"].n
                if not (T["x"].t is None and n < 2):
                    pe.wait_ge(x_free, T["x"].now() - 1)
                T["x"].up()
                return p_x[:, n % 2, :]

            def own_c():
                if not (T["c"].t is None and T["c"].n == 0):
                    pe.wait_ge(c_free, T["c"].now())
                T["c"].up()

            def blocks(source, n_blocks, product, between=None):
                groups = n_blocks // 4
                copied = []

                def transposes(g):
                    bank = own_x()
                    copied.append((T["x"].now(), (T["x"].n - 1) % 2))
                    for i in range(4):
                        last = nc.tensor.transpose(bank[:, i * P:(i + 1) * P],
                                                   source[:, (4 * g + i) * P:(4 * g + i + 1) * P], ident)
                    last.then_inc(x_ready, 1)

                def products(g):
                    value, buffer = copied[g]
                    pe.wait_ge(x_free, value)
                    for i in range(4):
                        last = product(4 * g + i, pt[:, buffer, i * P:(i + 1) * P])
                    last.then_inc(pt_used, 1)

                transposes(0)
                if groups > 1:
                    transposes(1)
                if between:
                    between()
                for g in range(groups):
                    products(g)
                    if g + 2 < groups:
                        transposes(g + 2)
                pe.wait_ge(pt_used, T["x"].now() + BUFFERS)

            def graph_logits(t, p, chunks):
                j, par = p % GH, (p // GH) % 2
                if j == 0 and 0 in chunks:
                    pe.wait_ge(mask_ready, t * 2 + (p // GH + 2))
                for c in chunks:
                    if not (isinstance(t, int) and t == 0 and p == -GH and c < 2):
                        pe.wait_ge(l_free, nth(t, GH + p, 4, c) - 2)
                    cols = slice(c * BANK, (c + 1) * BANK)
                    nc.tensor.matmul(p_l[c % 2], src_t[:, j, :], r_dst[:, cols], start=True, stop=False)
                    nc.tensor.matmul(p_l[c % 2], ident_bf, mask[par][:, cols], start=False, stop=True).then_inc(l_ready, 1)

            def graph_out(t, p, between=None):
                j = p % GH
                pe.wait_ge(gexp_ready, nth(t, GH + p))
                own_c()
                blocks(u[p % 2], NT, lambda m, block_t: nc.tensor.matmul(
                    p_c[:, 0:GD], block_t, h_all[:, m, j * GD:(j + 1) * GD], start=(m == 0), stop=(m == NT - 1)),
                    between)
                pe.sem_inc(c_ready, 1)
                pe.sem_inc(u_free, 1)

            def xn2_transpose(t):
                pe.wait_ge(xn2_ready, t + 1)
                own_c()
                nc.tensor.transpose(p_c[:, 0:P], xn2[:], ident).then_inc(c_ready, 1)
                pe.wait_ge(c_free, T["c"].now())

            def similarity(c):
                own_c()
                nc.tensor.matmul(p_c[:], xn2_t[:], wcomb[:, c * BANK:(c + 1) * BANK],
                                 start=True, stop=True).then_inc(c_ready, 1)

            def keys_transpose(t, h):
                pe.wait_ge(acc_ready, nth(t, h))
                own_c()
                nc.tensor.transpose(p_c[:, 0:P], acc[:, h % 2, 0:D], ident).then_inc(c_ready, 1)

            def scores(t, h, chunks):
                pe.wait_ge(c_free, T["c"].now())
                for c in range(chunks):
                    bank = p_s[:, c * BANK:(c + 1) * BANK]
                    nc.tensor.matmul(bank, q_t[:, h % MH, :], k_t[:, c, h % MH, :], start=True, stop=(c < chunks - 1))
                at = (t - (h < 0) - 4 * (chunks - 1)) * (-P) + (P + 3 * P)
                nc.tensor.matmul(bank, ident_bf, cstb[:, bass.ds(at, BANK)], start=False, stop=True).then_inc(s_ready, 1)

            def attend(t, h, chunks):
                pe.wait_ge(aexp_ready, nth(t, h))
                pe.wait_ge(kv_ready, nth(t, h) + BUFFERS)
                if not (isinstance(t, int) and t == 0 and h == 0):
                    pe.wait_ge(y_free, nth(t, h) - 1)
                blocks(prob, 4 * chunks, lambda m, block_t: nc.tensor.matmul(
                    p_o[:, 0:P], v[:, m, h % MH, :], block_t, start=(m == 0), stop=(m == 4 * chunks - 1)))
                pe.sem_inc(ot_ready, 1)

            def project(t, h):
                pe.wait_ge(otc_ready, nth(t, h))
                nc.tensor.matmul(p_o[:, P:2 * P], o_t[:], wo_s[:, h % MH, :], start=True, stop=True).then_inc(y_ready, 1)

            graph_logits(0, -GH, range(4))
            for p in range(GH):
                graph_logits(0, p + 1 - GH, range(4) if p < GH - 1 else range(2))
                graph_out(0, p - GH)
            xn2_transpose(0)
            for c in range(2):
                similarity(c)
            pe.wait_ge(ld_late, 64)
            pe.wait_ge(pool_zero, 2)
            settle(T)

            def body(t, first, pieces, nxt):
                ended = 0 < first < NT // 2
                for h in range(MH):
                    def between():
                        if h < pieces:
                            graph_logits(t, h, (2, 3))

                    if h - 1 < pieces if h else ended:
                        graph_out(t, h - 1, between)
                    else:
                        between()
                    if first or h > 0:
                        keys_transpose(t, h - 1)
                    if first or h > 1:
                        attend(t, h - 2, chunks_of(first, h - 2))
                    if first or h > 0:
                        scores(t, h - 1, chunks_of(first, h - 1))
                    if first or h > 1:
                        project(t, h - 2)
                    if h == 0:
                        for b in range(2):
                            own_c()
                            for i in range(4):
                                last = nc.tensor.matmul(p_c[:, i * P:(i + 1) * P],
                                                        wq_s[:, (4 * b + i) * D:(4 * b + i + 1) * D], xn2_t[:],
                                                        start=True, stop=True)
                            last.then_inc(c_ready, 1)
                    if h == 5 and nxt:
                        xn2_transpose(t + 1)
                    if h % 2 and (h < 4 or nxt):
                        similarity((h + 3) // 2 % 4)
                    if h + 1 < pieces or pieces == MH:
                        graph_logits(t, h + 1, (0, 1))

            over_tiles(pe, T, body)
            keys_transpose(NT, -1)
            attend(NT, -2, NT // 4)
            scores(NT, -1, NT // 4)
            project(NT, -2)
            attend(NT, -1, NT // 4)
            project(NT, -1)

        @block.vector
        def _(dve):
            T = tallies()
            step = [0]

            def mark(ins):
                step[0] += 1
                ins.then_inc(dve_step, 1)
                return step[0]

            def link(ins):
                dve.wait_ge(dve_step, mark(ins))

            def restart():
                dve.nop(nofuse=True)
                dve.wait_ge(dve_step, step[0])
                dve.sem_clear(dve_step)
                step[0] = 0

            dve.sem_inc(sim_free, BUFFERS)
            dve.sem_inc(row_free, RING_PARTS)
            dve.sem_inc(kv_ready, BUFFERS)
            link(nc.vector.memset(eps[:], LN_EPS))
            link(nc.vector.memset(wrow[:, :, :], 0.0))
            dve.wait_ge(ld_x, 16)
            for m in range(NT):
                link(nc.vector.bn_stats(stat[:], x1[:, m, :]))
                link(nc.vector.bn_aggr(mvx[:, m, :], stat[:]))
            dve.sem_inc(pro_dve, 1)
            dve.wait_ge(pro_act, 6)
            link(nc.vector.reciprocal(stdx[:], stdx[:]))
            for m in range(NT):
                ins = nc.vector.tensor_scalar(xn[:, m * P:(m + 1) * P], x1[:, m, :], mvx[:, m, 0:1], stdx[:, m:m + 1],
                                              ALU.subtract, ALU.mult)
            ins.then_inc(pro_dve, 1)
            dve.wait_ge(pro_pe, 5)
            link(nc.vector.tensor_scalar(wa_s, p_o[:, 0:8], ALPHA, None, ALU.mult))
            for s in range(2):
                for i in range(3):
                    ins = nc.vector.tensor_copy(
                        wrow[:, s, :].rearrange("p (j r) -> p j r", j=GH)[:, :, 3 * s + i],
                        wa_s[:, 4 * s:4 * s + 4])
            ins.then_inc(pro_dve, 1)
            dve.wait_ge(ld_c, 48)
            for s, (dest, cols) in enumerate(((r_src, src_cols), (r_dst, dst_cols))):
                for b in range(4):
                    dve.wait_ge(pro_pe, 9 + 4 * s + b + 1)
                    whole = p_s[:, b * BANK:(b + 1) * BANK]
                    link(nc.vector.tensor_copy(part, whole))
                    link(nc.vector.scalar_tensor_tensor(resid, part, cols[0], whole, ALU.mult, ALU.add))
                    link(nc.vector.tensor_copy(part, resid))
                    link(nc.vector.scalar_tensor_tensor(resid, part, cols[1], resid, ALU.mult, ALU.add))
                    nc.vector.tensor_scalar(dest[:, b * BANK:(b + 1) * BANK], resid, cols[2], None,
                                            ALU.add).then_inc(pro_dve, 1)
                    dve.wait_ge(pro_dve, 3 + 4 * s + b + 1)

            def graph_start(g, par):
                dve.wait_ge(adj_in, g * 16 + 16)
                link(nc.vector.tensor_scalar(mask[par], adj_s, 0.0, MASKED, ALU.is_le, ALU.mult))
                dve.sem_inc(adj_free, 1)
                for j in range(GH):
                    last = mark(nc.vector.tensor_scalar(src_t[:, j, :], r_src[:, bass.ds(g * P, P)], head_cols[j], None,
                                                        ALU.mult))
                dve.wait_ge(dve_step, last)
                dve.sem_inc(mask_ready, 1)

            def graph_piece(t, p, chunks):
                b = p % 2
                for c in chunks:
                    if c == 0:
                        dve.wait_ge(u_free, nth(t, GH + p))
                    dve.wait_ge(relu_ready, nth(t, GH + p, 4, c))
                    dve.nop(nofuse=True)
                    nc.vector.tensor_tensor_reduce(
                        u[b][:, c * BANK:(c + 1) * BANK], relu[:, c % 2, :], p_l[c % 2],
                        1.0, LOWEST, ALU.add, ALU.max, umax[:, c:c + 1]).then_inc(l_free, 1)
                if 3 in chunks:
                    dve.wait_ge(l_free, nth(t, GH + p, 4, 3))
                    nc.vector.tensor_reduce(neg_umax[:, b:b + 1], umax[:], AX_X, ALU.max, negate=True).then_inc(u_ready, 1)

            def norm_stats(source):
                link(nc.vector.bn_stats(stat[:], source))
                nc.vector.bn_aggr(mv[:], stat[:]).then_inc(var_ready, 1)

            def norm_apply(out, source):
                dve.wait_ge(std_ready, T["norm"].up())
                link(nc.vector.reciprocal(std[:, 1:2], std[:, 0:1]))
                return nc.vector.tensor_scalar(out, source, mv[:, 0:1], std[:, 1:2], ALU.subtract, ALU.mult)

            flat = gout[:].rearrange("p j d -> p (j d)")

            def graph_end_a(g, par):
                dve.wait_ge(gout_ready, g * GH + GH)
                link(nc.vector.reciprocal(grec[:], gsum[:, par, :]))
                link(nc.vector.tensor_tensor(gout[:], gout[:], grec[:].unsqueeze(2).to_broadcast([P, GH, GD]), ALU.mult))
                norm_stats(flat)

            def graph_end_b(g):
                link(norm_apply(flat, flat))
                link(nc.vector.tensor_tensor(flat, flat, gam[:], ALU.mult))
                link(nc.vector.tensor_tensor(flat, flat, bet[:], ALU.add))
                link(nc.vector.tensor_tensor(x1[:, g, :], x1[:, g, :], flat, ALU.add))

            def front_b(t):
                norm_apply(xn2[:], x1[:, t, :]).then_inc(xn2_ready, 1)

            def choose_a(t, h):
                if h % 2 == 0:
                    dve.wait_ge(sim_ready, t * (MH // 2) + (h // 2 + 1))
                dve.nop(nofuse=True)
                s = [sim[:, (h // 2) % 2, h % 2, half, :] for half in range(2)]
                value, index = best[:, 0], best[:, 1]
                m = [mark(nc.vector.max(value[:, f, 0:8], s[f])) for f in range(2)]
                for f in range(2):
                    dve.wait_ge(dve_step, m[f])
                    mark(nc.vector.max_index(besti[:, f, 0:8], value[:, f, 0:8], s[f]))
                m = [mark(nc.vector.match_replace(rest[:, f, :], value[:, f, 0:8], s[f], LOWEST)) for f in range(2)]
                for f in range(2):
                    dve.wait_ge(dve_step, m[f])
                    m[f] = mark(nc.vector.max(value[:, f, 8:16], rest[:, f, :]))
                for f in range(2):
                    dve.wait_ge(dve_step, m[f])
                    m[f] = mark(nc.vector.max_index(besti[:, f, 8:16], value[:, f, 8:16], rest[:, f, :]))
                if h % 2 == 1:
                    dve.sem_inc(sim_free, 1)
                dve.wait_ge(dve_step, m[1])
                mark(nc.vector.tensor_scalar(index[:, 0, :], besti[:, 0, :], 0.0, None, ALU.add))
                link(nc.vector.tensor_scalar(index[:, 1, :], besti[:, 1, :], float(NKEYS), None, ALU.mult))
                at = 0
                for i0, ni, nj in RECTS:
                    last = mark(nc.vector.tensor_tensor(
                        pair[:, :, at:at + ni * nj].rearrange("p c (i j) -> p c i j", i=ni),
                        best[:, :, 0, i0:i0 + ni].unsqueeze(3).to_broadcast([P, 2, ni, nj]),
                        best[:, :, 1, 0:nj].unsqueeze(2).to_broadcast([P, 2, ni, nj]), ALU.add))
                    at += ni * nj
                dve.wait_ge(dve_step, last)
                b = h % 2
                sums = pair[:, 0, :]
                link(nc.vector.max(top[:, b, 0:8], sums))
                mark(nc.vector.max_index(pos[:, 0:8], top[:, b, 0:8], sums))
                mark(nc.vector.tensor_scalar(neg_top[:, b:b + 1], top[:, b, 0:1], -1.0, None, ALU.mult))
                link(nc.vector.match_replace(prest[:], top[:, b, 0:8], sums, LOWEST))
                link(nc.vector.max(top[:, b, 8:16], prest[:]))
                nc.vector.max_index(pos[:, 8:16], top[:, b, 8:16], prest[:]).then_inc(top_ready, 1)

            def choose_b(t, h):
                b, w = h % 2, h % MH
                dve.wait_ge(pos_ready, nth(t, h))
                link(nc.vector.tensor_tensor(hot[:], posx[:], iota[:], ALU.is_equal))
                link(nc.vector.tensor_tensor(hot[:], hot[:], pidx[:].unsqueeze(1).to_broadcast([P, TOPK, NC]), ALU.mult))
                dve.wait_ge(wsum_ready, nth(t, h))
                mark(nc.vector.reciprocal(wrec[:, b:b + 1], wsum[:, b:b + 1]))
                with nc.allow_low_precision(reason="whole numbers below 2**14, one of them not zero"):
                    link(nc.vector.tensor_reduce(idx[:, w, :], hot[:], AX_X, ALU.add))
                nc.vector.tensor_scalar(idx[:, w, :], idx[:, w, :], float(w * NKEYS * NKEYS), None,
                                        ALU.add).then_inc(idx_ready, 1)

            done = [None, None]

            def combine(t, h, part):
                even, odd = acc[:, h % 2, :], acc_odd[:]
                if part == 0:
                    dve.wait_ge(kv_ready, nth(t, h) + (BUFFERS - 2))
                    dve.wait_ge(w_ready, nth(t, h))
                for k in range(4 * part, 4 * part + 4):
                    to = odd if k % 2 else even
                    dve.wait_ge(row_in[k], nth(t, h) * 16)
                    if k > 1:
                        dve.wait_ge(*done[k % 2])
                    if k < 2:
                        ins = nc.vector.tensor_scalar(to, rows[:, k, :], wgt[:, h, k:k + 1], None, ALU.mult)
                    else:
                        ins = nc.vector.scalar_tensor_tensor(to, rows[:, k, :], wgt[:, h, k:k + 1], to,
                                                             ALU.mult, ALU.add)
                    if k % 4 == 3:
                        ins.then_inc(row_free, 1)
                        done[1] = (row_free, nth(t, h, RING_PARTS, part) + RING_PARTS)
                    else:
                        done[k % 2] = (dve_step, mark(ins))
                if part == 3:
                    dve.wait_ge(*done[1])
                    nc.vector.tensor_tensor(even, even, odd, ALU.add).then_inc(acc_ready, 1)
                    dve.wait_ge(acc_ready, nth(t, h))

            def row_max(t, h, chunks):
                b = h % 2
                dve.wait_ge(s_ready, nth(t, h))
                nc.vector.tensor_reduce(neg_max[:, b:b + 1], p_s[:, 0:chunks * BANK], AX_X, ALU.max,
                                        negate=True).then_inc(max_ready, 1)

            def add_head(t, h):
                b, tile = h % 2, t - (h < 0)
                dve.wait_ge(aexp_ready, nth(t, h))
                link(nc.vector.reciprocal(prec[:], psum_row[:, b:b + 1]))
                dve.wait_ge(y_ready, nth(t, h))
                nc.vector.scalar_tensor_tensor(x1[:, tile, :], p_o[:, P:2 * P], prec[:], x1[:, tile, :],
                                               ALU.mult, ALU.add).then_inc(y_free, 1)
                dve.wait_ge(y_free, nth(t, h))

            graph_start(0, 1)
            dve.wait_ge(pro_act, 14)
            for p in range(GH):
                graph_piece(0, p - GH, range(4))
            graph_start(1, 0)
            dve.wait_ge(ld_late, 64)
            graph_end_a(0, 1)
            graph_end_b(0)
            norm_stats(x1[:, 0, :])
            front_b(0)
            for h in range(2):
                choose_a(0, h)
                choose_b(0, h)
            settle(T)
            restart()

            def body(t, first, pieces, nxt):
                ended = 0 < first < NT // 2
                for h in range(MH):
                    end = 2 * t if h == 0 and ended else 2 * t + 1 if h == GH and pieces else None
                    if first or h > 1:
                        row_max(t, h - 2, chunks_of(first, h - 2))
                    if h < pieces:
                        graph_piece(t, h, (0, 1))
                    if first or h > 2:
                        add_head(t, h - 3)
                        if h == 2:
                            dve.sem_inc(res_ready, 1)
                    combine(t, h, 0)
                    if h < pieces:
                        graph_piece(t, h, (2, 3))
                    if pieces == MH and (h == GH - 1 or h == MH - 1):
                        graph_start(2 * t + (2 if h < GH else 3), int(h < GH))
                    if h == 5 and nxt:
                        norm_stats(x1[:, t + 1, :])
                    if h < 6 or nxt:
                        choose_a(t, h + 2)
                    combine(t, h, 1)
                    if h == 5 and nxt:
                        front_b(t + 1)
                    if end is not None:
                        graph_end_a(end, int(h == 0))
                    if h < 6 or nxt:
                        choose_b(t, h + 2)
                    combine(t, h, 2)
                    combine(t, h, 3)
                    if end is not None:
                        graph_end_b(end)
                    if first == NT // 2 - 1 and h >= GH:
                        for i in (2 * (h - GH), 2 * (h - GH) + 1):
                            mark(nc.vector.memset(k_t[:, 2:4, i, :], 0.0))
                            link(nc.vector.memset(v[:, NT // 2 + i, :, :], 0.0))
                T["x"].n, T["c"].n = T["x"].per, T["c"].per
                restart()

            over_tiles(dve, T, body)
            row_max(NT, -2, NT // 4)
            add_head(NT, -3)
            add_head(NT, -2)
            row_max(NT, -1, NT // 4)
            add_head(NT, -1)
            dve.sem_inc(res_ready, 1)


def constants(np):
    c = np.zeros((P, C_END), np.float32)
    c[:, C_IDENT:C_IDENT + P] = np.eye(P)
    r = np.arange(P) % 32
    for s in range(2):
        third = r - 3 * s
        c[:, C_THIRDS + 3 * s] = -1.0 * ((third == 1) | (third == 2))
        c[:, C_THIRDS + 3 * s + 1] = -1.0 * (third == 2)
        c[:, C_THIRDS + 3 * s + 2] = (r < 6) & ((third < 0) | (third > 2))
    for j in range(GH):
        c[:, C_HEADS + j] = np.arange(P) // 32 == j
    b = np.zeros((P, CB_END), np.float32)
    b[:, 0:P] = np.eye(P)
    col = np.arange(BANK + 3 * P)[None, :] - 3 * P
    b[:, P:CB_END] = np.where(col <= np.arange(P)[:, None], 0.0, LOWEST)
    return c, b


def kernel(**inputs):
    import numpy as np
    import concourse.bacc as _bacc
    from concourse.bass_utils import run_bass_kernel_spmd as _run

    f = {n: np.asarray(a) for n, a in inputs.items()}
    a = f["L0_gnn_a"]
    a_blk = np.zeros((P, 2 * GH), a.dtype)
    for j in range(GH):
        a_blk[j * GD:(j + 1) * GD, j] = a[0:GD, 0]
        a_blk[j * GD:(j + 1) * GD, GH + j] = a[GD:2 * GD, 0]
    const, const_bf = constants(np)
    arrays = dict(
        x=f["x"], adj=f["adj"], w=f["L0_gnn_W"], w_t=f["L0_gnn_W"].T, a_blk=a_blk,
        gamma=f["L0_gnn_gamma"], beta=f["L0_gnn_beta"],
        wqpk=f["L0_ffn_Wq_pk"].reshape(D, 2, MH, DKEY).transpose(3, 2, 1, 0).reshape(DKEY, N),
        keys=f["L0_ffn_pk_keys"].transpose(3, 2, 0, 1).reshape(DKEY, N),
        wq=f["L0_ffn_Wq"],
        kv=np.concatenate([f["L0_ffn_keys_table"], f["L0_ffn_values_table"]], axis=1),
        wo=f["L0_ffn_Wo"], const=const, const_bf=const_bf,
        iota16=np.tile(np.arange(NC, dtype=np.uint16), (P, TOPK)),
    )
    arrays = {n: np.ascontiguousarray(v) for n, v in arrays.items()}
    nc = _bacc.Bacc("TRN2", target_bir_lowering=False, num_devices=1)
    args = [nc.dram_tensor(n, v.shape, mybir.dt.from_np(v.dtype), kind="ExternalInput").ap()
            for n, v in arrays.items()]
    args.append(nc.dram_tensor("out", (N, D), F32, kind="ExternalOutput").ap())
    build(nc, *args)
    r = _run(nc, [arrays], core_ids=[0])
    return r.results[0]["out"]
```

```python
from contextlib import ExitStack

import concourse.bass as bass
from concourse import mybir

F32 = mybir.dt.float32
BF16 = mybir.dt.bfloat16
U32 = mybir.dt.uint32
U16 = mybir.dt.uint16
ALU = mybir.AluOpType
ACT = mybir.ActivationFunctionType
AX_X = mybir.AxisListType.X

P = 128
N = 2048
NT = N // P
D = 128
GH, GD = 4, 32
MH = 8
NKEYS = 128
DKEY = 64
TOPK = 16
BANK = 512
ALPHA = 0.2
LN_EPS = 1e-5
MASKED = -9.0e15
LOWEST = -3.0e38
RECTS = [(0, 1, 16), (1, 1, 8), (2, 2, 5), (4, 4, 3), (8, 8, 1)]
NC = sum(a * b for _, a, b in RECTS)
SPANS = [(0, 1, 8, 1), (1, 4, 8, 1), (4, 5, 8, 1), (5, 6, 8, 1), (6, 7, 8, 1), (7, 8, 4, 1), (8, 9, 0, 1), (9, 12, 0, 1),
         (12, 13, 0, 1), (13, 15, 0, 1), (15, 16, 0, 0)]
C_IDENT, C_THIRDS, C_HEADS, C_END = 0, P, P + 4, P + 4 + GH
CB_END = P + BANK + 3 * P


class Tally:

    def __init__(self, start=0):
        self.base, self.n, self.t, self.first, self.per = start, 0, None, 0, 0

    def enter(self, t, first, per):
        self.t, self.first, self.per = t, first, per

    def leave(self, bodies):
        assert self.n in (0, self.per), (self.n, self.per)
        self.base += self.per * bodies
        self.n, self.t = 0, None

    def up(self, k=1):
        self.n += k
        return self.now()

    def now(self):
        if self.t is None:
            return self.base + self.n
        if isinstance(self.t, int):
            return self.base + self.n + (self.t - self.first) * self.per
        return self.t * self.per + (self.base + self.n - self.first * self.per)


def per_body(first, pieces, nxt):
    outs = pieces + int(0 < first < NT // 2) - (pieces == MH)
    stored = MH - (first == 0)
    chunks = sum(((first + (h - 2) // MH) // 4 + 1) for h in range(MH) if first or h > 1)
    sims = 2 + 2 * nxt
    c = outs + stored + 2 + sims + nxt
    norms = int(0 < first < NT // 2) + (pieces > 0) + nxt
    return dict(x=4 * outs + chunks, c=c, norm=norms)


PROLOGUE = dict(x=4 * GH, c=GH + 3, norm=2)
BUFFERS = 2
RING_PARTS = 4


def build(nc, x, adj, w, w_t, a_blk, gamma, beta, wqpk, keys, wq, kv, wo, const, const_bf, iota16, out):
    with ExitStack() as ctx:
        def sb(name, shape, dt=F32):
            return ctx.enter_context(nc.sbuf_tensor(name, shape, dt))

        def ps(name, shape):
            return ctx.enter_context(nc.psum_tensor(name, shape, F32))

        def sem(name):
            return ctx.enter_context(nc.semaphore(name))

        k_t = sb("k_t", [P, 4, MH, BANK])
        v = sb("v", [P, NT, MH, D])
        rows = sb("rows", [P, TOPK, 2 * D])
        wcomb = sb("wcomb", [P, MH * 2 * NKEYS])
        wq_s = sb("wq_s", [P, MH * D])
        wo_s = sb("wo_s", [P, MH, D])
        x1 = sb("x1", [P, NT, D])
        prob = sb("prob", [P, N])
        pt = sb("pt", [P, 2, BANK])
        sim = sb("sim", [P, 2, 2, 2, NKEYS])
        q_t = sb("q_t", [P, MH, P])
        cst = sb("cst", [P, C_END])
        cstb = sb("cstb", [P, CB_END], BF16)
        iota = sb("iota", [P, TOPK, NC], U16)
        gam = sb("gam", [P, D])
        bet = sb("bet", [P, D])
        acc = sb("acc", [P, 2, 2 * D])
        acc_odd = sb("acc_odd", [P, 2 * D])
        o_t = sb("o_t", [P, P])
        xn2 = sb("xn2", [P, D])
        xn2_t = sb("xn2_t", [P, P])
        gout = sb("gout", [P, GH, GD])
        best = sb("best", [P, 2, 2, TOPK])
        besti = sb("besti", [P, 2, TOPK], U32)
        rest = sb("rest", [P, 2, NKEYS])
        pair = sb("pair", [P, 2, NC])
        prest = sb("prest", [P, NC])
        top = sb("top", [P, 2, TOPK])
        pos = sb("pos", [P, TOPK], U32)
        posx = sb("posx", [P, TOPK, NC], U16)
        pidx = sb("pidx", [P, NC], U16)
        hot = sb("hot", [P, TOPK, NC], U16)
        idx = sb("idx", [P, MH, TOPK], U32)
        wgt = sb("wgt", [P, MH, TOPK])
        stat = sb("stat", [P, 6])
        mv = sb("mv", [P, 2])
        std = sb("std", [P, 2])
        eps = sb("eps", [P, 1])
        umax = sb("umax", [P, 4])
        neg_umax = sb("neg_umax", [P, 2])
        gsum = sb("gsum", [P, 2, GH])
        grec = sb("grec", [P, GH])
        neg_top = sb("neg_top", [P, 2])
        wsum = sb("wsum", [P, 2])
        wrec = sb("wrec", [P, 2])
        neg_max = sb("neg_max", [P, 2])
        max_half = sb("max_half", [P, 2])
        psum_row = sb("psum_row", [P, 2, 2])
        prec = sb("prec", [P, 1])
        mvx = sb("mvx", [P, NT, 2])
        stdx = sb("stdx", [P, NT])
        k_hi = k_t[:, 2:4].rearrange("p q h c -> p (q h c)")
        v_hi = v[:, NT // 2:NT].rearrange("p t h d -> p (t h d)")
        xn_t = k_hi[:, 0:N]
        h_all = k_hi[:, N:2 * N].rearrange("p (t d) -> p t d", t=NT)
        r_src = k_hi[:, 2 * N:2 * N + N // 2].bitcast(BF16)
        r_dst = k_hi[:, 2 * N + N // 2:3 * N].bitcast(BF16)
        spare = k_hi[:, 3 * N:4 * N]
        wrow = spare[:, 0:P]
        src_t = spare[:, 2 * P:4 * P].bitcast(BF16).rearrange("p (j n) -> p j n", j=GH)
        w_s = spare[:, 4 * P:5 * P]
        ab_s = spare[:, 5 * P:5 * P + 8]
        wa_s = spare[:, 5 * P + 8:5 * P + 16]
        part = spare[:, 6 * P:8 * P].bitcast(BF16)
        relu = spare[:, 8 * P:16 * P].rearrange("p (a b) -> p a b", a=2)
        stats_x = spare[:, 5 * P + 16:5 * P + 16 + 6 * NT].rearrange("p (t s) -> p t s", t=NT)
        wt_s = spare[:, 8 * P:9 * P]
        u = [v_hi[:, 0:N], v_hi[:, N:2 * N]]
        adj_s = v_hi[:, 2 * N:3 * N]
        mask = [v_hi[:, 3 * N:3 * N + N // 2].bitcast(BF16), v_hi[:, 3 * N + N // 2:4 * N].bitcast(BF16)]
        wqpk_s = v_hi[0:DKEY, 0:N]
        keys_s = v_hi[0:DKEY, N:2 * N]
        xn = prob
        resid = pt[:, 0, :]
        cstb_f32 = sim[:].rearrange("p a b c d -> p (a b c d)")

        ident = cst[:, C_IDENT:C_IDENT + P]
        ident_bf = cstb[:, 0:P]
        head_cols = [cst[:, C_HEADS + j:C_HEADS + j + 1] for j in range(GH)]
        minus_1, minus_2, is_src, is_dst = (cst[:, C_THIRDS + i:C_THIRDS + i + 1] for i in range(4))

        p_s = ps("p_s", [P, 4 * BANK])
        p_l = [p_s[:, (2 + i) * BANK:(3 + i) * BANK] for i in range(2)]
        p_x = ps("p_x", [P, 2, BANK])
        p_c = ps("p_c", [P, BANK])
        p_o = ps("p_o", [P, BANK])

        names = list(PROLOGUE)
        adj_free, mask_ready = sem("adj_free"), sem("mask_ready")
        l_ready, relu_ready, l_free = sem("l_ready"), sem("relu_ready"), sem("l_free")
        u_ready, gexp_ready, u_free, gout_ready = sem("u_ready"), sem("gexp_ready"), sem("u_free"), sem("gout_ready")
        var_ready, std_ready, xn2_ready = sem("var_ready"), sem("std_ready"), sem("xn2_ready")
        sim_ready, sim_free, top_ready, pos_ready = sem("sim_ready"), sem("sim_free"), sem("top_ready"), sem("pos_ready")
        wsum_ready, w_ready, idx_ready, row_free = sem("wsum_ready"), sem("w_ready"), sem("idx_ready"), sem("row_free")
        acc_ready, kv_ready, s_ready, max_ready = sem("acc_ready"), sem("kv_ready"), sem("s_ready"), sem("max_ready")
        aexp_ready, ot_ready, otc_ready = sem("aexp_ready"), sem("ot_ready"), sem("otc_ready")
        y_ready, y_free, res_ready = sem("y_ready"), sem("y_free"), sem("res_ready")
        x_ready, x_free, pt_used, c_ready, c_free = sem("x_ready"), sem("x_free"), sem("pt_used"), sem("c_ready"), sem("c_free")
        row_in = [sem(f"row_in{k}") for k in range(TOPK)]
        adj_in = sem("adj_in")
        ld_x, ld_w, ld_pk, ld_c, ld_late = sem("ld_x"), sem("ld_w"), sem("ld_pk"), sem("ld_c"), sem("ld_late")
        out_done = sem("out_done")
        pool_zero = sem("pool_zero")
        dve_step = sem("dve_step")
        pro_pe, pro_act, pro_dve = sem("pro_pe"), sem("pro_act"), sem("pro_dve")

        x_v = x.rearrange("(t p) d -> p t d", p=P)
        out_v = out.rearrange("(t p) d -> p t d", p=P)
        adj_v = adj.rearrange("(t p) m -> p t m", p=P)

        def tallies():
            return {n: Tally() for n in names}

        def settle(T):
            for n in names:
                assert T[n].n in (0, PROLOGUE[n]), (n, T[n].n)
                T[n].base, T[n].n = PROLOGUE[n], 0

        def over_tiles(eng, T, body):
            for first, end, pieces, nxt in SPANS:
                per = per_body(first, pieces, nxt)

                def one(t):
                    for n in names:
                        T[n].enter(t, first, per[n])
                    body(t, first, pieces, nxt)

                if end - first == 1:
                    one(first)
                else:
                    with eng.Fori(first, end) as t:
                        one(t)
                for n in names:
                    T[n].leave(end - first)

        def chunks_of(first, h):
            return (first - (h < 0)) // 4 + 1

        def nth(t, h, parts=1, k=0):
            return t * (MH * parts) + (h * parts + k + 1)

        def halves(chunks):
            cut = (chunks + 1) // 2 * BANK
            return [(0, cut), (cut, chunks * BANK)] if chunks > 1 else [(0, BANK)]

        block = ctx.enter_context(nc.Block())

        @block.sync
        def _(sp):
            T = tallies()
            sp.dma_start(x1[:], x_v).then_inc(ld_x, 16)
            sp.dma_start(wt_s, w_t).then_inc(ld_w, 16)
            sp.dma_start(ab_s, a_blk).then_inc(ld_w, 16)
            sp.dma_start(w_s, w).then_inc(ld_w, 16)
            sp.dma_start(adj_s, adj_v[:, 0, :]).then_inc(adj_in, 16)
            sp.dma_start(wq_s[:], wq).then_inc(ld_late, 16)
            sp.dma_start(wo_s[:], wo.rearrange("(h d) n -> d h n", d=D)).then_inc(ld_late, 16)
            sp.dma_start(gam[:], gamma.partition_broadcast(P)).then_inc(ld_late, 16)
            sp.dma_start(bet[:], beta.partition_broadcast(P)).then_inc(ld_late, 16)

            for g in range(1, 3):
                sp.wait_ge(adj_free, g)
                sp.dma_start(adj_s, adj_v[:, g, :]).then_inc(adj_in, 16)

            def body(t, first, pieces, nxt):
                if first:
                    sp.wait_ge(res_ready, t)
                    sp.dma_start(out_v[:, t - 1, :], x1[:, t - 1, :]).then_inc(out_done, 16)
                if pieces == MH:
                    for g in range(3, 5):
                        if first == 6 and g == 4:
                            continue
                        sp.wait_ge(adj_free, 2 * t + g)
                        sp.dma_start(adj_s, adj_v[:, 2 * t + g, :]).then_inc(adj_in, 16)

            over_tiles(sp, T, body)
            sp.wait_ge(res_ready, NT)
            sp.dma_start(out_v[:, NT - 1, :], x1[:, NT - 1, :]).then_inc(out_done, 16)
            sp.wait_ge(out_done, 16 * NT)

        @block.gpsimd
        def _(pool):
            nc.gpsimd.memset(k_t[:, 0:2].rearrange("p q h c -> p (q h c)"), 0.0).then_inc(pool_zero, 1)
            nc.gpsimd.memset(v[:, 0:NT // 2].rearrange("p t h d -> p (t h d)"), 0.0).then_inc(pool_zero, 1)
            with pool.Fori(0, NT) as t:
                for h in range(MH):
                    pool.wait_ge(idx_ready, nth(t, h))
                    pool.nop(nofuse=True)
                    for k in range(TOPK):
                        if k % 4 == 0:
                            pool.wait_ge(row_free, nth(t, h, RING_PARTS, k // 4))
                            pool.nop(nofuse=True)
                        nc.gpsimd.indirect_dma_start(
                            out=rows[:, k, :], out_offset=None, in_=kv,
                            in_offset=bass.IndirectOffsetOnAxis(ap=idx[:, h, k:k + 1], axis=0),
                        ).then_inc(row_in[k], 16)

        @block.scalar
        def _(act):
            T = tallies()
            act.dma_start(wqpk_s, wqpk).then_inc(ld_pk, 16)
            act.dma_start(keys_s, keys).then_inc(ld_pk, 16)
            act.dma_start(cst[:], const).then_inc(ld_c, 16)
            act.dma_start(cstb_f32, const_bf).then_inc(ld_c, 16)
            act.dma_start(iota[:].rearrange("p a b -> p (a b)"), iota16).then_inc(ld_c, 16)
            act.wait_ge(pro_dve, 1)
            nc.scalar.activation(stdx[:], mvx[:, :, 1], ACT.Sqrt, bias=eps[:]).then_inc(pro_act, 1)
            for b in range(4):
                act.wait_ge(pro_pe, b + 1)
                nc.scalar.activation(wcomb[:, b * BANK:(b + 1) * BANK], p_s[:, b * BANK:(b + 1) * BANK],
                                     ACT.Copy).then_inc(pro_act, 1)
            for b in range(4):
                act.wait_ge(pro_pe, 5 + b + 1)
                nc.scalar.activation(xn_t[:, b * BANK:(b + 1) * BANK], p_s[:, b * BANK:(b + 1) * BANK],
                                     ACT.Copy).then_inc(pro_act, 1)
            act.wait_ge(ld_c, 48)
            nc.scalar.activation(cstb[:], cstb_f32, ACT.Copy).then_inc(pro_act, 1)
            for b in range(4):
                act.wait_ge(pro_pe, 13 + b + 1)
                nc.scalar.activation(h_all[:, 4 * b:4 * b + 4, :],
                                     p_s[:, b * BANK:(b + 1) * BANK].rearrange("p (t d) -> p t d", t=4),
                                     ACT.Copy).then_inc(pro_act, 1)

            def take_c(out, in_, scale=1.0):
                act.wait_ge(c_ready, T["c"].up())
                nc.scalar.activation(out, in_, ACT.Copy, scale=scale).then_inc(c_free, 1)

            def tell(semaphore):
                act.wait_ge(c_free, T["c"].now())
                act.sem_inc(semaphore, 1)

            def take_x():
                n = T["x"].n
                act.wait_ge(x_ready, T["x"].up())
                act.wait_ge(pt_used, T["x"].now() + (BUFFERS - 2))
                nc.scalar.activation(pt[:, n % 2, :], p_x[:, n % 2, :], ACT.Copy).then_inc(x_free, 1)

            def graph_relu(t, p, chunks):
                for c in chunks:
                    act.wait_ge(l_ready, nth(t, GH + p, 4, c))
                    nc.scalar.activation(relu[:, c % 2, :], p_l[c % 2], ACT.Relu,
                                         scale=1.0 / ALPHA - 1.0).then_inc(relu_ready, 1)

            def graph_exp(t, p):
                b, j = p % 2, p % GH
                par = 1 if t is None else p // GH
                act.wait_ge(u_ready, nth(0, p) if t is None else nth(t, GH + p))
                nc.scalar.activation(u[b], u[b], ACT.Exp, bias=neg_umax[:, b:b + 1],
                                     accum_out=gsum[:, par, j:j + 1]).then_inc(gexp_ready, 1)

            def graph_take(p):
                take_c(gout[:, p % GH, :], p_c[:, 0:GD])
                tell(gout_ready)

            def sqrt_step():
                act.wait_ge(var_ready, T["norm"].up())
                nc.scalar.activation(std[:, 0:1], mv[:, 1:2], ACT.Sqrt, bias=eps[:]).then_inc(std_ready, 1)

            def choice_copies(t, h):
                b, w = h % 2, h % MH
                act.wait_ge(top_ready, nth(t, h))
                nc.scalar.activation(posx[:], pos[:].unsqueeze(2).to_broadcast([P, TOPK, NC]), ACT.Copy)
                nc.scalar.activation(pidx[:], pair[:, 1, :], ACT.Copy).then_inc(pos_ready, 1)
                nc.scalar.activation(wgt[:, w, :], top[:, b, :], ACT.Exp, bias=neg_top[:, b:b + 1],
                                     accum_out=wsum[:, b:b + 1]).then_inc(wsum_ready, 1)

            def weights(t, h):
                b, w = h % 2, h % MH
                act.wait_ge(idx_ready, nth(t, h))
                nc.scalar.activation(wgt[:, w, :], wgt[:, w, :], ACT.Copy, scale=wrec[:, b:b + 1]).then_inc(w_ready, 1)

            def attend_exp(t, h, chunks):
                b = h % 2
                act.wait_ge(max_ready, nth(t, h))
                for i, (start, end) in enumerate(halves(chunks)):
                    nc.scalar.activation(prob[:, start:end], p_s[:, start:end], ACT.Exp, bias=neg_max[:, b:b + 1],
                                         accum_out=psum_row[:, b, i:i + 1]).then_inc(aexp_ready, 1 if chunks > 1 else 2)

            def attend_copies(t, h, chunks, between=None):
                for g in range(chunks):
                    take_x()
                    if g == min(2, chunks) - 1 and between:
                        between()
                act.wait_ge(ot_ready, nth(t, h))
                nc.scalar.activation(o_t[:], p_o[:, 0:P], ACT.Copy).then_inc(otc_ready, 1)

            def store_kv(t, h, quad):
                tile = t - (h < 0)
                take_c(k_t[:, quad, h % MH, bass.ds((tile - 4 * quad) * P, P)], p_c[:, 0:P])
                act.wait_ge(acc_ready, nth(t, h))
                nc.scalar.activation(v[:, tile, h % MH, :], acc[:, h % 2, D:2 * D], ACT.Copy).then_inc(kv_ready, 1)

            def take_sim(t, c):
                act.wait_ge(sim_free, t * (MH // 2) + (c + 1))
                take_c(sim[:, c % 2].rearrange("p a b c -> p (a b c)"), p_c[:, :])
                tell(sim_ready)

            graph_relu(0, -GH, range(4))
            for p in range(GH):
                graph_exp(None, p)
                graph_relu(0, p + 1 - GH, range(4) if p < GH - 1 else range(2))
                for _ in range(4):
                    take_x()
                graph_take(p)
            sqrt_step()
            sqrt_step()
            take_c(xn2_t[:], p_c[:, 0:P])
            for c in range(2):
                take_sim(0, c)
            for h in range(2):
                choice_copies(0, h)
                weights(0, h)
            settle(T)

            def body(t, first, pieces, nxt):
                ended = 0 < first < NT // 2
                for h in range(MH):
                    out_now = h - 1 < pieces if h else ended
                    norm_now = (h == 0 and ended) or (h == GH and pieces)
                    choose = h < 6 or nxt
                    if out_now:
                        take_x()
                        take_x()
                    if first or h > 1:
                        attend_exp(t, h - 2, chunks_of(first, h - 2))
                    if h < pieces:
                        graph_relu(t, h, (2, 3))
                    if out_now:
                        take_x()
                        take_x()
                        graph_take(h - 1)
                    if h == 5 and nxt:
                        sqrt_step()
                    if first or h > 0:
                        store_kv(t, h - 1, chunks_of(first, h - 1) - 1)

                    def between():
                        if choose:
                            choice_copies(t, h + 2)

                    if norm_now or not (first or h > 1):
                        between()
                    if first or h > 1:
                        attend_copies(t, h - 2, chunks_of(first, h - 2), None if norm_now else between)
                    if norm_now:
                        sqrt_step()
                    if h < pieces:
                        graph_exp(t, h)
                    if choose:
                        weights(t, h + 2)
                    if h == 0:
                        for b in range(2):
                            take_c(q_t[:, 4 * b:4 * b + 4, :].rearrange("p a b -> p (a b)"), p_c[:, :],
                                   scale=float(D) ** -0.5)
                    if h == 5 and nxt:
                        take_c(xn2_t[:], p_c[:, 0:P])
                    if h % 2 and (h < 4 or nxt):
                        take_sim(t, (h + 3) // 2)
                    if h + 1 < pieces or pieces == MH:
                        graph_relu(t, h + 1, (0, 1))

            over_tiles(act, T, body)
            attend_exp(NT, -2, NT // 4)
            store_kv(NT, -1, NT // 4 - 1)
            attend_copies(NT, -2, NT // 4)
            attend_exp(NT, -1, NT // 4)
            attend_copies(NT, -1, NT // 4)

        @block.tensor
        def _(pe):
            T = tallies()
            pe.sem_inc(u_free, BUFFERS)
            pe.sem_inc(pt_used, BUFFERS)
            pe.wait_ge(ld_pk, 32)
            for b in range(4):
                for i in range(4 * b, 4 * b + 4):
                    last = nc.tensor.matmul(p_s[:, i * P:(i + 1) * P], wqpk_s[:, i * P:(i + 1) * P],
                                            keys_s[:, i * P:(i + 1) * P], start=True, stop=True)
                last.then_inc(pro_pe, 1)
            pe.wait_ge(ld_w, 48)
            nc.tensor.matmul(p_o[:, 0:8], wt_s, ab_s, start=True, stop=True).then_inc(pro_pe, 1)
            pe.wait_ge(pro_dve, 2)
            pe.wait_ge(ld_c, 48)
            for b in range(4):
                pe.wait_ge(pro_act, 1 + b + 1)
                for i in range(4 * b, 4 * b + 4):
                    last = nc.tensor.transpose(p_s[:, i * P:(i + 1) * P], xn[:, i * P:(i + 1) * P], ident)
                last.then_inc(pro_pe, 1)
            pe.wait_ge(pro_dve, 3)
            for b in range(4):
                pe.wait_ge(pro_act, 5 + b + 1)
                nc.tensor.matmul(p_s[:, b * BANK:(b + 1) * BANK], wrow, xn_t[:, b * BANK:(b + 1) * BANK],
                                 start=True, stop=True).then_inc(pro_pe, 1)
            for b in range(4):
                pe.wait_ge(pro_dve, 3 + b + 1)
                for i in range(4 * b, 4 * b + 4):
                    last = nc.tensor.matmul(p_s[:, i * P:(i + 1) * P], xn_t[:, i * P:(i + 1) * P], w_s,
                                            start=True, stop=True)
                last.then_inc(pro_pe, 1)
            pe.wait_ge(pro_act, 14)

            def own_x():
                n = T["x"].n
                if not (T["x"].t is None and n < 2):
                    pe.wait_ge(x_free, T["x"].now() - 1)
                T["x"].up()
                return p_x[:, n % 2, :]

            def own_c():
                if not (T["c"].t is None and T["c"].n == 0):
                    pe.wait_ge(c_free, T["c"].now())
                T["c"].up()

            def blocks(source, n_blocks, product, between=None, ready={}):
                groups = n_blocks // 4
                copied = []

                def transposes(g):
                    if g in ready:
                        pe.wait_ge(aexp_ready, ready[g])
                    bank = own_x()
                    copied.append((T["x"].now(), (T["x"].n - 1) % 2))
                    for i in range(4):
                        last = nc.tensor.transpose(bank[:, i * P:(i + 1) * P],
                                                   source[:, (4 * g + i) * P:(4 * g + i + 1) * P], ident)
                    last.then_inc(x_ready, 1)

                def products(g):
                    value, buffer = copied[g]
                    pe.wait_ge(x_free, value)
                    for i in range(4):
                        last = product(4 * g + i, pt[:, buffer, i * P:(i + 1) * P])
                    last.then_inc(pt_used, 1)

                transposes(0)
                if groups > 1:
                    transposes(1)
                if between:
                    between()
                for g in range(groups):
                    products(g)
                    if g + 2 < groups:
                        transposes(g + 2)
                pe.wait_ge(pt_used, T["x"].now() + BUFFERS)

            def graph_logits(t, p, chunks):
                j, par = p % GH, (p // GH) % 2
                if j == 0 and 0 in chunks:
                    pe.wait_ge(mask_ready, t * 2 + (p // GH + 2))
                for c in chunks:
                    if not (isinstance(t, int) and t == 0 and p == -GH and c < 2):
                        pe.wait_ge(l_free, nth(t, GH + p, 4, c) - 2)
                    cols = slice(c * BANK, (c + 1) * BANK)
                    nc.tensor.matmul(p_l[c % 2], src_t[:, j, :], r_dst[:, cols], start=True, stop=False)
                    nc.tensor.matmul(p_l[c % 2], ident_bf, mask[par][:, cols], start=False, stop=True).then_inc(l_ready, 1)

            def graph_out(t, p, between=None):
                j = p % GH
                pe.wait_ge(gexp_ready, nth(t, GH + p))
                own_c()
                blocks(u[p % 2], NT, lambda m, block_t: nc.tensor.matmul(
                    p_c[:, 0:GD], block_t, h_all[:, m, j * GD:(j + 1) * GD], start=(m == 0), stop=(m == NT - 1)),
                    between)
                pe.sem_inc(c_ready, 1)
                pe.sem_inc(u_free, 1)

            def xn2_transpose(t):
                pe.wait_ge(xn2_ready, t + 1)
                own_c()
                nc.tensor.transpose(p_c[:, 0:P], xn2[:], ident).then_inc(c_ready, 1)
                pe.wait_ge(c_free, T["c"].now())

            def similarity(c):
                own_c()
                nc.tensor.matmul(p_c[:], xn2_t[:], wcomb[:, c * BANK:(c + 1) * BANK],
                                 start=True, stop=True).then_inc(c_ready, 1)

            def keys_transpose(t, h):
                pe.wait_ge(acc_ready, nth(t, h))
                own_c()
                nc.tensor.transpose(p_c[:, 0:P], acc[:, h % 2, 0:D], ident).then_inc(c_ready, 1)

            def scores(t, h, chunks):
                pe.wait_ge(c_free, T["c"].now())
                for c in range(chunks):
                    bank = p_s[:, c * BANK:(c + 1) * BANK]
                    last = nc.tensor.matmul(bank, q_t[:, h % MH, :], k_t[:, c, h % MH, :], start=True,
                                            stop=(c < chunks - 1))
                    if chunks > 2 and c == 1:
                        last.then_inc(s_ready, 1)
                at = (t - (h < 0) - 4 * (chunks - 1)) * (-P) + (P + 3 * P)
                nc.tensor.matmul(bank, ident_bf, cstb[:, bass.ds(at, BANK)], start=False, stop=True).then_inc(s_ready, 1 if chunks > 2 else 2)

            def attend(t, h, chunks):
                pe.wait_ge(kv_ready, nth(t, h) + BUFFERS)
                if not (isinstance(t, int) and t == 0 and h == 0):
                    pe.wait_ge(y_free, nth(t, h) - 1)
                blocks(prob, 4 * chunks, lambda m, block_t: nc.tensor.matmul(
                    p_o[:, 0:P], v[:, m, h % MH, :], block_t, start=(m == 0), stop=(m == 4 * chunks - 1)),
                    ready={0: nth(t, h, 2, 0), (chunks + 1) // 2: nth(t, h, 2, 1)} if chunks > 1 else {0: nth(t, h, 2, 1)})
                pe.sem_inc(ot_ready, 1)

            def project(t, h):
                pe.wait_ge(otc_ready, nth(t, h))
                nc.tensor.matmul(p_o[:, P:2 * P], o_t[:], wo_s[:, h % MH, :], start=True, stop=True).then_inc(y_ready, 1)

            graph_logits(0, -GH, range(4))
            for p in range(GH):
                graph_logits(0, p + 1 - GH, range(4) if p < GH - 1 else range(2))
                graph_out(0, p - GH)
            xn2_transpose(0)
            for c in range(2):
                similarity(c)
            pe.wait_ge(ld_late, 64)
            pe.wait_ge(pool_zero, 2)
            settle(T)

            def body(t, first, pieces, nxt):
                ended = 0 < first < NT // 2
                for h in range(MH):
                    def between():
                        if h < pieces:
                            graph_logits(t, h, (2, 3))

                    if h - 1 < pieces if h else ended:
                        graph_out(t, h - 1, between)
                    else:
                        between()
                    if first or h > 0:
                        keys_transpose(t, h - 1)
                    if first or h > 1:
                        attend(t, h - 2, chunks_of(first, h - 2))
                    if first or h > 0:
                        scores(t, h - 1, chunks_of(first, h - 1))
                    if first or h > 1:
                        project(t, h - 2)
                    if h == 0:
                        for b in range(2):
                            own_c()
                            for i in range(4):
                                last = nc.tensor.matmul(p_c[:, i * P:(i + 1) * P],
                                                        wq_s[:, (4 * b + i) * D:(4 * b + i + 1) * D], xn2_t[:],
                                                        start=True, stop=True)
                            last.then_inc(c_ready, 1)
                    if h == 5 and nxt:
                        xn2_transpose(t + 1)
                    if h % 2 and (h < 4 or nxt):
                        similarity((h + 3) // 2 % 4)
                    if h + 1 < pieces or pieces == MH:
                        graph_logits(t, h + 1, (0, 1))

            over_tiles(pe, T, body)
            keys_transpose(NT, -1)
            attend(NT, -2, NT // 4)
            scores(NT, -1, NT // 4)
            project(NT, -2)
            attend(NT, -1, NT // 4)
            project(NT, -1)

        @block.vector
        def _(dve):
            T = tallies()
            step = [0]

            def mark(ins):
                step[0] += 1
                ins.then_inc(dve_step, 1)
                return step[0]

            def link(ins):
                dve.wait_ge(dve_step, mark(ins))

            def restart():
                dve.nop(nofuse=True)
                dve.wait_ge(dve_step, step[0])
                dve.sem_clear(dve_step)
                step[0] = 0

            dve.sem_inc(sim_free, BUFFERS)
            dve.sem_inc(row_free, RING_PARTS)
            dve.sem_inc(kv_ready, BUFFERS)
            link(nc.vector.memset(eps[:], LN_EPS))
            link(nc.vector.memset(wrow, 0.0))
            dve.wait_ge(ld_x, 16)
            for m in range(NT):
                last = mark(nc.vector.bn_stats(stats_x[:, m, :], x1[:, m, :]))
            dve.wait_ge(dve_step, last)
            for m in range(NT):
                last = mark(nc.vector.bn_aggr(mvx[:, m, :], stats_x[:, m, :]))
            dve.wait_ge(dve_step, last)
            dve.sem_inc(pro_dve, 1)
            dve.wait_ge(pro_act, 1)
            link(nc.vector.reciprocal(stdx[:], stdx[:]))
            for m in range(NT):
                ins = nc.vector.tensor_scalar(xn[:, m * P:(m + 1) * P], x1[:, m, :], mvx[:, m, 0:1], stdx[:, m:m + 1],
                                              ALU.subtract, ALU.mult)
            ins.then_inc(pro_dve, 1)
            dve.wait_ge(pro_pe, 5)
            link(nc.vector.tensor_scalar(wa_s, p_o[:, 0:8], ALPHA, None, ALU.mult))
            for s in range(2):
                for i in range(3):
                    ins = nc.vector.tensor_copy(
                        wrow.rearrange("p (j r) -> p j r", j=GH)[:, :, 3 * s + i],
                        wa_s[:, 4 * s:4 * s + 4])
            ins.then_inc(pro_dve, 1)
            dve.wait_ge(ld_c, 48)
            for b in range(4):
                dve.wait_ge(pro_pe, 9 + b + 1)
                whole, cols = p_s[:, b * BANK:(b + 1) * BANK], slice(b * BANK, (b + 1) * BANK)
                link(nc.vector.tensor_copy(part, whole))
                link(nc.vector.scalar_tensor_tensor(resid, part, minus_1, whole, ALU.mult, ALU.add))
                link(nc.vector.tensor_copy(part, resid))
                link(nc.vector.scalar_tensor_tensor(resid, part, minus_2, resid, ALU.mult, ALU.add))
                mark(nc.vector.tensor_scalar(r_src[:, cols], resid, is_src, is_dst, ALU.mult, ALU.add))
                nc.vector.tensor_scalar(r_dst[:, cols], resid, is_dst, is_src, ALU.mult, ALU.add).then_inc(pro_dve, 1)
                dve.wait_ge(pro_dve, 3 + b + 1)

            def graph_start(g, par):
                dve.wait_ge(adj_in, g * 16 + 16)
                link(nc.vector.tensor_scalar(mask[par], adj_s, 0.0, MASKED, ALU.is_le, ALU.mult))
                dve.sem_inc(adj_free, 1)
                for j in range(GH):
                    last = mark(nc.vector.tensor_scalar(src_t[:, j, :], r_src[:, bass.ds(g * P, P)], head_cols[j], None,
                                                        ALU.mult))
                dve.wait_ge(dve_step, last)
                dve.sem_inc(mask_ready, 1)

            def graph_piece(t, p, chunks):
                b = p % 2
                for c in chunks:
                    if c == 0:
                        dve.wait_ge(u_free, nth(t, GH + p))
                    dve.wait_ge(relu_ready, nth(t, GH + p, 4, c))
                    dve.nop(nofuse=True)
                    nc.vector.tensor_tensor_reduce(
                        u[b][:, c * BANK:(c + 1) * BANK], relu[:, c % 2, :], p_l[c % 2],
                        1.0, LOWEST, ALU.add, ALU.max, umax[:, c:c + 1]).then_inc(l_free, 1)
                if 3 in chunks:
                    dve.wait_ge(l_free, nth(t, GH + p, 4, 3))
                    nc.vector.tensor_reduce(neg_umax[:, b:b + 1], umax[:], AX_X, ALU.max, negate=True).then_inc(u_ready, 1)

            def norm_stats(source):
                link(nc.vector.bn_stats(stat[:], source))
                nc.vector.bn_aggr(mv[:], stat[:]).then_inc(var_ready, 1)

            def norm_apply(out, source):
                dve.wait_ge(std_ready, T["norm"].up())
                link(nc.vector.reciprocal(std[:, 1:2], std[:, 0:1]))
                return nc.vector.tensor_scalar(out, source, mv[:, 0:1], std[:, 1:2], ALU.subtract, ALU.mult)

            flat = gout[:].rearrange("p j d -> p (j d)")

            def graph_end_a(g, par):
                dve.wait_ge(gout_ready, g * GH + GH)
                link(nc.vector.reciprocal(grec[:], gsum[:, par, :]))
                link(nc.vector.tensor_tensor(gout[:], gout[:], grec[:].unsqueeze(2).to_broadcast([P, GH, GD]), ALU.mult))
                norm_stats(flat)

            def graph_end_b(g):
                link(norm_apply(flat, flat))
                link(nc.vector.tensor_tensor(flat, flat, gam[:], ALU.mult))
                link(nc.vector.tensor_tensor(flat, flat, bet[:], ALU.add))
                link(nc.vector.tensor_tensor(x1[:, g, :], x1[:, g, :], flat, ALU.add))

            def front_b(t):
                norm_apply(xn2[:], x1[:, t, :]).then_inc(xn2_ready, 1)

            done = [None, None]

            def combine(t, h, rows_now):
                even, odd = acc[:, h % 2, :], acc_odd[:]
                for k in rows_now:
                    if k == 0:
                        dve.wait_ge(kv_ready, nth(t, h) + (BUFFERS - 2))
                        dve.wait_ge(w_ready, nth(t, h))
                    to = odd if k % 2 else even
                    dve.wait_ge(row_in[k], nth(t, h) * 16)
                    if k > 1:
                        dve.wait_ge(*done[k % 2])
                    elif k == 1 and not (isinstance(t, int) and t == 0 and h == 0):
                        dve.wait_ge(acc_ready, nth(t, h) - 1)
                    if k < 2:
                        ins = nc.vector.tensor_scalar(to, rows[:, k, :], wgt[:, h, k:k + 1], None, ALU.mult)
                    else:
                        ins = nc.vector.scalar_tensor_tensor(to, rows[:, k, :], wgt[:, h, k:k + 1], to,
                                                             ALU.mult, ALU.add)
                    if k % 4 == 3:
                        ins.then_inc(row_free, 1)
                        done[1] = (row_free, nth(t, h, RING_PARTS, k // 4) + RING_PARTS)
                    else:
                        done[k % 2] = (dve_step, mark(ins))

            def combine_end(t, h):
                even = acc[:, h % 2, :]
                dve.wait_ge(*done[1])
                nc.vector.tensor_tensor(even, even, acc_odd[:], ALU.add).then_inc(acc_ready, 1)

            def choose_a(t, h, fill=False):
                def row(k):
                    if fill:
                        combine(t, h - 2, (k,))

                if h % 2 == 0:
                    dve.wait_ge(sim_ready, t * (MH // 2) + (h // 2 + 1))
                dve.nop(nofuse=True)
                s = [sim[:, (h // 2) % 2, h % 2, half, :] for half in range(2)]
                value, index = best[:, 0], best[:, 1]
                m = [mark(nc.vector.max(value[:, f, 0:8], s[f])) for f in range(2)]
                for f in range(2):
                    dve.wait_ge(dve_step, m[f])
                    mark(nc.vector.max_index(besti[:, f, 0:8], value[:, f, 0:8], s[f]))
                m = [mark(nc.vector.match_replace(rest[:, f, :], value[:, f, 0:8], s[f], LOWEST)) for f in range(2)]
                for f in range(2):
                    dve.wait_ge(dve_step, m[f])
                    m[f] = mark(nc.vector.max(value[:, f, 8:16], rest[:, f, :]))
                for f in range(2):
                    dve.wait_ge(dve_step, m[f])
                    m[f] = mark(nc.vector.max_index(besti[:, f, 8:16], value[:, f, 8:16], rest[:, f, :]))
                if h % 2 == 1:
                    dve.sem_inc(sim_free, 1)
                row(4)
                dve.wait_ge(dve_step, m[1])
                mark(nc.vector.tensor_scalar(index[:, 0, :], besti[:, 0, :], 0.0, None, ALU.add))
                last = mark(nc.vector.tensor_scalar(index[:, 1, :], besti[:, 1, :], float(NKEYS), None, ALU.mult))
                row(5)
                dve.wait_ge(dve_step, last)
                at = 0
                for i0, ni, nj in RECTS:
                    last = mark(nc.vector.tensor_tensor(
                        pair[:, :, at:at + ni * nj].rearrange("p c (i j) -> p c i j", i=ni),
                        best[:, :, 0, i0:i0 + ni].unsqueeze(3).to_broadcast([P, 2, ni, nj]),
                        best[:, :, 1, 0:nj].unsqueeze(2).to_broadcast([P, 2, ni, nj]), ALU.add))
                    at += ni * nj
                row(6)
                dve.wait_ge(dve_step, last)
                b = h % 2
                sums = pair[:, 0, :]
                link(nc.vector.max(top[:, b, 0:8], sums))
                last = mark(nc.vector.match_replace(prest[:], top[:, b, 0:8], sums, LOWEST))
                mark(nc.vector.max_index(pos[:, 0:8], top[:, b, 0:8], sums))
                mark(nc.vector.tensor_scalar(neg_top[:, b:b + 1], top[:, b, 0:1], -1.0, None, ALU.mult))
                dve.wait_ge(dve_step, last)
                last = mark(nc.vector.max(top[:, b, 8:16], prest[:]))
                row(7)
                dve.wait_ge(dve_step, last)
                nc.vector.max_index(pos[:, 8:16], top[:, b, 8:16], prest[:]).then_inc(top_ready, 1)

            def choose_b(t, h, fill=False):
                def row(k):
                    if fill:
                        combine(t, h - 2, (k,))

                b, w = h % 2, h % MH
                dve.wait_ge(pos_ready, nth(t, h))
                last = mark(nc.vector.tensor_tensor(hot[:], posx[:], iota[:], ALU.is_equal))
                row(11)
                dve.wait_ge(dve_step, last)
                last = mark(nc.vector.tensor_tensor(hot[:], hot[:], pidx[:].unsqueeze(1).to_broadcast([P, TOPK, NC]),
                                                    ALU.mult))
                row(12)
                dve.wait_ge(wsum_ready, nth(t, h))
                mark(nc.vector.reciprocal(wrec[:, b:b + 1], wsum[:, b:b + 1]))
                dve.wait_ge(dve_step, last)
                with nc.allow_low_precision(reason="whole numbers below 2**14, one of them not zero"):
                    last = mark(nc.vector.tensor_reduce(idx[:, w, :], hot[:], AX_X, ALU.add))
                row(13)
                dve.wait_ge(dve_step, last)
                nc.vector.tensor_scalar(idx[:, w, :], idx[:, w, :], float(w * NKEYS * NKEYS), None,
                                        ALU.add).then_inc(idx_ready, 1)
                row(14)

            def row_max_half(t, h, chunks, i):
                start, end = halves(chunks)[i]
                dve.wait_ge(s_ready, nth(t, h, 2, i))
                return mark(nc.vector.tensor_reduce(max_half[:, i:i + 1], p_s[:, start:end], AX_X, ALU.max))

            def row_max(t, h, chunks):
                b = h % 2
                if chunks > 2:
                    dve.wait_ge(dve_step, row_max_half(t, h, chunks, 1))
                    nc.vector.tensor_reduce(neg_max[:, b:b + 1], max_half[:], AX_X, ALU.max,
                                            negate=True).then_inc(max_ready, 1)
                else:
                    dve.wait_ge(s_ready, nth(t, h, 2, 1))
                    nc.vector.tensor_reduce(neg_max[:, b:b + 1], p_s[:, 0:chunks * BANK], AX_X, ALU.max,
                                            negate=True).then_inc(max_ready, 1)

            def add_head(t, h, chunks):
                b, tile = h % 2, t - (h < 0)
                dve.wait_ge(aexp_ready, nth(t, h, 2, 1))
                if chunks > 1:
                    link(nc.vector.tensor_tensor(prec[:], psum_row[:, b, 0:1], psum_row[:, b, 1:2], ALU.add))
                    link(nc.vector.reciprocal(prec[:], prec[:]))
                else:
                    link(nc.vector.reciprocal(prec[:], psum_row[:, b, 0:1]))
                dve.wait_ge(y_ready, nth(t, h))
                nc.vector.scalar_tensor_tensor(x1[:, tile, :], p_o[:, P:2 * P], prec[:], x1[:, tile, :],
                                               ALU.mult, ALU.add).then_inc(y_free, 1)
                dve.wait_ge(y_free, nth(t, h))

            graph_start(0, 1)
            dve.wait_ge(pro_act, 14)
            for p in range(GH):
                graph_piece(0, p - GH, range(4))
            graph_start(1, 0)
            dve.wait_ge(ld_late, 64)
            graph_end_a(0, 1)
            graph_end_b(0)
            norm_stats(x1[:, 0, :])
            front_b(0)
            for h in range(2):
                choose_a(0, h)
                choose_b(0, h)
            settle(T)
            restart()

            def body(t, first, pieces, nxt):
                ended = 0 < first < NT // 2
                for h in range(MH):
                    end = 2 * t if h == 0 and ended else 2 * t + 1 if h == GH and pieces else None
                    if first or h > 1:
                        row_max(t, h - 2, chunks_of(first, h - 2))
                    if h < pieces:
                        graph_piece(t, h, (0, 1))
                    if first or h > 2:
                        add_head(t, h - 3, chunks_of(first, h - 3))
                        if h == 2:
                            dve.sem_inc(res_ready, 1)
                    combine(t, h, range(0, 4))
                    if h == 5 and nxt:
                        norm_stats(x1[:, t + 1, :])
                    if h < 6 or nxt:
                        choose_a(t, h + 2, fill=True)
                    else:
                        combine(t, h, range(4, 8))
                    if h < pieces:
                        graph_piece(t, h, (2, 3))
                    if pieces == MH and (h == GH - 1 or h == MH - 1):
                        graph_start(2 * t + (2 if h < GH else 3), int(h < GH))
                    combine(t, h, range(8, 11))
                    if h == 5 and nxt:
                        front_b(t + 1)
                    if end is not None:
                        graph_end_a(end, int(h == 0))
                    if h < 6 or nxt:
                        choose_b(t, h + 2, fill=True)
                    else:
                        combine(t, h, range(11, 15))
                    combine(t, h, (15,))
                    combine_end(t, h)
                    if (first or h > 0) and chunks_of(first, h - 1) > 2:
                        row_max_half(t, h - 1, chunks_of(first, h - 1), 0)
                    if end is not None:
                        graph_end_b(end)
                    if first == NT // 2 - 1 and h >= GH:
                        for i in (2 * (h - GH), 2 * (h - GH) + 1):
                            mark(nc.vector.memset(k_t[:, 2:4, i, :], 0.0))
                            link(nc.vector.memset(v[:, NT // 2 + i, :, :], 0.0))
                T["x"].n, T["c"].n = T["x"].per, T["c"].per
                restart()

            over_tiles(dve, T, body)
            row_max(NT, -2, NT // 4)
            add_head(NT, -3, NT // 4)
            add_head(NT, -2, NT // 4)
            row_max_half(NT, -1, NT // 4, 0)
            row_max(NT, -1, NT // 4)
            add_head(NT, -1, NT // 4)
            dve.sem_inc(res_ready, 1)


def constants(np):
    c = np.zeros((P, C_END), np.float32)
    c[:, C_IDENT:C_IDENT + P] = np.eye(P)
    r = np.arange(P) % 32
    third = r % 3
    c[:, C_THIRDS] = -1.0 * ((r < 6) & (third > 0))
    c[:, C_THIRDS + 1] = -1.0 * ((r < 6) & (third > 1))
    c[:, C_THIRDS + 2] = r < 3
    c[:, C_THIRDS + 3] = (r >= 3) & (r < 6)
    for j in range(GH):
        c[:, C_HEADS + j] = np.arange(P) // 32 == j
    b = np.zeros((P, CB_END), np.float32)
    b[:, 0:P] = np.eye(P)
    col = np.arange(BANK + 3 * P)[None, :] - 3 * P
    b[:, P:CB_END] = np.where(col <= np.arange(P)[:, None], 0.0, LOWEST)
    return c, b


def kernel(**inputs):
    import numpy as np
    import concourse.bacc as _bacc
    from concourse.bass_utils import run_bass_kernel_spmd as _run

    f = {n: np.asarray(a) for n, a in inputs.items()}
    a = f["L0_gnn_a"]
    a_blk = np.zeros((P, 2 * GH), a.dtype)
    for j in range(GH):
        a_blk[j * GD:(j + 1) * GD, j] = a[0:GD, 0]
        a_blk[j * GD:(j + 1) * GD, GH + j] = a[GD:2 * GD, 0]
    const, const_bf = constants(np)
    arrays = dict(
        x=f["x"], adj=f["adj"], w=f["L0_gnn_W"], w_t=f["L0_gnn_W"].T, a_blk=a_blk,
        gamma=f["L0_gnn_gamma"], beta=f["L0_gnn_beta"],
        wqpk=f["L0_ffn_Wq_pk"].reshape(D, 2, MH, DKEY).transpose(3, 2, 1, 0).reshape(DKEY, N),
        keys=f["L0_ffn_pk_keys"].transpose(3, 2, 0, 1).reshape(DKEY, N),
        wq=f["L0_ffn_Wq"],
        kv=np.concatenate([f["L0_ffn_keys_table"], f["L0_ffn_values_table"]], axis=1),
        wo=f["L0_ffn_Wo"], const=const, const_bf=const_bf,
        iota16=np.tile(np.arange(NC, dtype=np.uint16), (P, TOPK)),
    )
    arrays = {n: np.ascontiguousarray(v) for n, v in arrays.items()}
    nc = _bacc.Bacc("TRN2", target_bir_lowering=False, num_devices=1)
    args = [nc.dram_tensor(n, v.shape, mybir.dt.from_np(v.dtype), kind="ExternalInput").ap()
            for n, v in arrays.items()]
    args.append(nc.dram_tensor("out", (N, D), F32, kind="ExternalOutput").ap())
    build(nc, *args)
    r = _run(nc, [arrays], core_ids=[0])
    return r.results[0]["out"]
```
